# Optimizing a Trainium2 kernel written in Bass

```python
import numpy as np
import jax
import jax.numpy as jnp

def _softmax(x, axis=-1):
    return jax.nn.softmax(x, axis=axis)

def _gelu(x):
    return jax.nn.gelu(x, approximate=True)

def _silu(x):
    return jax.nn.silu(x)

def _sigmoid(x):
    return jax.nn.sigmoid(x)

def _layernorm(x, axis=-1, eps=1e-05):
    m = jnp.mean(x, axis=axis, keepdims=True)
    v = jnp.var(x, axis=axis, keepdims=True)
    return (x - m) / jnp.sqrt(v + eps)

def _scatter_add(tgt, idx, src, axis=0):
    return tgt.at[idx].add(src)

def _segment_sum(src, seg, n):
    return jax.ops.segment_sum(src, seg, n)
kernel_name = 'mk_xattn_seq_d2_seqx_r4_9209bc'

def setup_inputs(seed: int=0):
    np.random.seed(seed)
    _w = jnp.asarray

    def _rec_inputs():
        import jax
        import jax.numpy as jnp
        _rk = jax.random.key(seed)
        x = 7.22e-05 + 1 * jax.random.normal(jax.random.fold_in(_rk, 1), (32, 256, 256), jnp.float32)
        _lenS = 256 - jax.random.randint(jax.random.fold_in(_rk, 7), (32,), 0, max(1, 256 // 4) + 1, jnp.int32)
        _lenS2 = 256 - jax.random.randint(jax.random.fold_in(_rk, 8), (32,), 0, max(1, 256 // 4) + 1, jnp.int32)
        _ctx_1024P = jax.random.normal(jax.random.fold_in(_rk, 11), (32, 16, 256), jnp.float32)
        _ctx_1024c = jax.random.dirichlet(jax.random.fold_in(_rk, 511), 0.3 * jnp.ones((16,), jnp.float32), (32, 256))
        _ctx_1024t = jnp.einsum('bsk,bkd->bsd', _ctx_1024c, _ctx_1024P)
        _ctx_1024t = _ctx_1024t * jax.lax.rsqrt(jnp.mean(jnp.square(_ctx_1024t)) + 1e-12) * 0.953939
        ctx_1024 = 4.13588e-05 + 0.999923 * (_ctx_1024t + 0.3 * jax.random.normal(jax.random.fold_in(_rk, 611), (32, 256, 256), jnp.float32))
        return (x, ctx_1024)
    x, ctx_1024 = _rec_inputs()

    def _L0_xattn_setup():
        import jax, jax.numpy as jnp
        import numpy as np
        NH = 16
        key = jax.random.key(seed)
        ks = jax.random.split(key, 5)
        B, N, D = (4, 512, 256)
        return {'tgt': jax.random.normal(ks[0], (B, N, D), dtype=jnp.float32), 'memory': jax.random.normal(ks[1], (B, N, D), dtype=jnp.float32), 'Wq': jax.random.normal(ks[2], (D, D), dtype=jnp.float32) * (1.0 / np.sqrt(D)), 'Wk': jax.random.normal(ks[3], (D, D), dtype=jnp.float32) * (1.0 / np.sqrt(D)), 'Wv': jax.random.normal(ks[4], (D, D), dtype=jnp.float32) * (1.0 / np.sqrt(D))}
    _L0_xattn_all = _L0_xattn_setup()
    _L0_xattn_in = {k: v for k, v in _L0_xattn_all.items() if k in ('Wq', 'Wk', 'Wv')}
    del _L0_xattn_all

    def _L1_xattn_setup():
        import jax, jax.numpy as jnp
        import numpy as np
        EMBED_DIM = 256
        LN_EPS = 1e-05

        def _layernorm(x, w, b):
            m = jnp.mean(x, axis=-1, keepdims=True)
            v = jnp.mean(jnp.square(x - m), axis=-1, keepdims=True)
            return (x - m) * jax.lax.rsqrt(v + LN_EPS) * w + b

        def _attention(q, k, v, scale):
            scores = jnp.einsum('bqd,bkd->bqk', q, k) * scale
            probs = jax.nn.softmax(scores, axis=-1)
            return jnp.einsum('bqk,bkd->bqd', probs, v)
        key = jax.random.key(seed)
        ks = jax.random.split(key, 16)
        B, SQ, SK, D, H = (8, 577, 13271, EMBED_DIM, 4)
        return {'input_features': jax.random.normal(ks[0], (B, SK, D), jnp.float32), 'query_feature': jax.random.normal(ks[1], (B, SQ, D), jnp.float32), 'norm1_w': jax.random.uniform(ks[2], (D,), jnp.float32, 0.5, 1.5), 'norm1_b': jax.random.normal(ks[3], (D,), jnp.float32) * 0.1, 'norm2_w': jax.random.uniform(ks[4], (D,), jnp.float32, 0.5, 1.5), 'norm2_b': jax.random.normal(ks[5], (D,), jnp.float32) * 0.1, 'norm3_w': jax.random.uniform(ks[6], (D,), jnp.float32, 0.5, 1.5), 'norm3_b': jax.random.normal(ks[7], (D,), jnp.float32) * 0.1, 'gamma1': jax.random.uniform(ks[8], (D,), jnp.float32, 0.5, 1.5), 'gamma2': jax.random.uniform(ks[9], (D,), jnp.float32, 0.5, 1.5), 'fc1_w': jax.random.normal(ks[10], (H, D), jnp.float32) * (1.0 / np.sqrt(D)), 'fc1_b': jax.random.normal(ks[11], (H,), jnp.float32) * 0.01, 'fc2_w': jax.random.normal(ks[12], (D, H), jnp.float32) * (1.0 / np.sqrt(H)), 'fc2_b': jax.random.normal(ks[13], (D,), jnp.float32) * 0.01}
    _L1_xattn_all = _L1_xattn_setup()
    _L1_xattn_in = {k: v for k, v in _L1_xattn_all.items() if k in ('norm1_w', 'norm1_b', 'norm2_w', 'norm2_b', 'norm3_w', 'norm3_b', 'gamma1', 'gamma2', 'fc1_w', 'fc1_b', 'fc2_w', 'fc2_b')}
    del _L1_xattn_all
    return {'x': x, 'ctx_1024': ctx_1024, 'L0_xattn_Wq': _L0_xattn_in['Wq'], 'L0_xattn_Wk': _L0_xattn_in['Wk'], 'L0_xattn_Wv': _L0_xattn_in['Wv'], 'L1_xattn_norm1_w': _L1_xattn_in['norm1_w'], 'L1_xattn_norm1_b': _L1_xattn_in['norm1_b'], 'L1_xattn_norm2_w': _L1_xattn_in['norm2_w'], 'L1_xattn_norm2_b': _L1_xattn_in['norm2_b'], 'L1_xattn_norm3_w': _L1_xattn_in['norm3_w'], 'L1_xattn_norm3_b': _L1_xattn_in['norm3_b'], 'L1_xattn_gamma1': _L1_xattn_in['gamma1'], 'L1_xattn_gamma2': _L1_xattn_in['gamma2'], 'L1_xattn_fc1_w': _L1_xattn_in['fc1_w'], 'L1_xattn_fc1_b': _L1_xattn_in['fc1_b'], 'L1_xattn_fc2_w': _L1_xattn_in['fc2_w'], 'L1_xattn_fc2_b': _L1_xattn_in['fc2_b']}

def reference(x, ctx_1024, L0_xattn_Wq, L0_xattn_Wk, L0_xattn_Wv, L1_xattn_norm1_w, L1_xattn_norm1_b, L1_xattn_norm2_w, L1_xattn_norm2_b, L1_xattn_norm3_w, L1_xattn_norm3_b, L1_xattn_gamma1, L1_xattn_gamma2, L1_xattn_fc1_w, L1_xattn_fc1_b, L1_xattn_fc2_w, L1_xattn_fc2_b):
    import jax
    import jax.numpy as jnp

    def _L0_xattn_ref(tgt, memory, Wq, Wk, Wv):
        import jax, jax.numpy as jnp
        import numpy as np
        NH = 16
        B, N, D = tgt.shape
        dk = D // NH
        scale = 1.0 / np.sqrt(dk)
        q = (tgt @ Wq.T).reshape(B, N, NH, dk).transpose(0, 2, 1, 3)
        k = (memory @ Wk.T).reshape(B, N, NH, dk).transpose(0, 2, 1, 3)
        v = (memory @ Wv.T).reshape(B, N, NH, dk).transpose(0, 2, 1, 3)
        scores = jnp.einsum('bhqd,bhkd->bhqk', q, k) * scale
        probs = jax.nn.softmax(scores, axis=-1)
        att = jnp.einsum('bhqk,bhkd->bhqd', probs, v)
        att = att.transpose(0, 2, 1, 3).reshape(B, N, D)
        tgt2 = att[0]
        return tgt + tgt2

    def _L1_xattn_ref(input_features, query_feature, norm1_w, norm1_b, norm2_w, norm2_b, norm3_w, norm3_b, gamma1, gamma2, fc1_w, fc1_b, fc2_w, fc2_b):
        import jax, jax.numpy as jnp
        import numpy as np
        EMBED_DIM = 256
        LN_EPS = 1e-05

        def _layernorm(x, w, b):
            m = jnp.mean(x, axis=-1, keepdims=True)
            v = jnp.mean(jnp.square(x - m), axis=-1, keepdims=True)
            return (x - m) * jax.lax.rsqrt(v + LN_EPS) * w + b

        def _attention(q, k, v, scale):
            scores = jnp.einsum('bqd,bkd->bqk', q, k) * scale
            probs = jax.nn.softmax(scores, axis=-1)
            return jnp.einsum('bqk,bkd->bqd', probs, v)
        scale = EMBED_DIM ** (-0.5)
        norm_X = _layernorm(input_features, norm1_w, norm1_b)
        norm_F_L = _layernorm(query_feature, norm2_w, norm2_b)
        attended = _attention(norm_F_L, norm_X, norm_X, scale)
        h = jax.nn.gelu(attended @ fc1_w.T + fc1_b, approximate=False)
        cross_attended = h @ fc2_w.T + fc2_b
        norm_cross = _layernorm(cross_attended, norm3_w, norm3_b)
        self_attended = _attention(norm_cross, norm_cross, norm_cross, scale)
        skip_connect = cross_attended + gamma1 * self_attended
        return norm_F_L + gamma2 * skip_connect
    x = _L0_xattn_ref(x, ctx_1024, L0_xattn_Wq, L0_xattn_Wk, L0_xattn_Wv)
    x = _L1_xattn_ref(ctx_1024, x, L1_xattn_norm1_w, L1_xattn_norm1_b, L1_xattn_norm2_w, L1_xattn_norm2_b, L1_xattn_norm3_w, L1_xattn_norm3_b, L1_xattn_gamma1, L1_xattn_gamma2, L1_xattn_fc1_w, L1_xattn_fc1_b, L1_xattn_fc2_w, L1_xattn_fc2_b)
    return x

_drawn_inputs = setup_inputs


def setup_inputs(seed=0):
    import zlib

    import numpy as np

    out = dict(_drawn_inputs(seed))
    spreads = {}
    factors = {'L1_xattn_fc1_b': 4.736}
    for name, (base, spread) in spreads.items():
        noise = np.random.default_rng([zlib.crc32(name.encode()), seed]).standard_normal(out[name].shape)
        drawn = base * np.exp(spread * noise) if base else spread * noise
        out[name] = jnp.asarray(drawn.astype(out[name].dtype))
    for name, factor in factors.items():
        out[name] = (out[name] * factor).astype(out[name].dtype)
    return out
```

```python
from contextlib import ExitStack

import concourse.bass as bass
from concourse import mybir

F32 = mybir.dt.float32
BF16 = mybir.dt.bfloat16
I32 = mybir.dt.int32
ALU = mybir.AluOpType
ACT = mybir.ActivationFunctionType
AX = mybir.AxisListType

P = 128
B = 32
N = 256
D = 256
NT = N // P
DC = D // P
TILES = B * NT
NH = 16
DK = D // NH
H = 4
U = H + 2
EPS = 1e-5
SCALE1 = float(D) ** -0.5
RSQRT_SEED = float(0x5F3759DF)
NEWTON = 3
NCHAIN = 9 + 3 * NEWTON
PARTS_L = (0, 0, 1, 1, 0, 2)
PARTS_R = (0, 1, 0, 1, 2, 0)
SLOT = 64
SU = 6 * U
CO = 2 * H + 2
SC = 6 * CO

COLS = {}
_n = 0
for _name, _w in (("w1", 2), ("b1", 2), ("w2", 2), ("b2", 2), ("w3", 2), ("b3", 2), ("g1", 2), ("g2", 2),
                  ("even", 1), ("odd", 1), ("fc1b", H), ("a5", DC * (H + 1)), ("fc1", DC * H)):
    COLS[_name] = (_n, _n + _w)
    _n += _w
NPAR = _n


def build(nc, x, ctx, x0t, c0t, wqt, wkt, wvt, params, out):
    stack = ExitStack()

    def sb(name, shape, dt=F32):
        return stack.enter_context(nc.sbuf_tensor(name, shape, dt))

    def sem(name):
        return stack.enter_context(nc.semaphore(name))

    bank = [stack.enter_context(nc.psum_tensor(f"bank{i}", [P, 512], F32)) for i in range(8)]

    def tiles(ap, w=256):
        return ap[:, 0:2 * w].rearrange("p (a b) -> p a b", a=2)

    par = sb("par", [P, NPAR])
    ident = sb("ident", [P, P])
    identb = sb("identb", [P, P], BF16)
    sel = sb("sel", [4, 4 * P], BF16)
    meanw = sb("meanw", [P, P])
    scalew = sb("scalew", [P, P])
    x0T, c0T = sb("x0T", [P, DC, N]), sb("c0T", [P, DC, N])
    wqT, wkT, wvT = (sb(n, [P, DC, D]) for n in ("wqT", "wkT", "wvT"))
    qT = sb("qT", [P, 2, N])
    kTm = sb("kTm", [P, 2, 2, N])
    v1 = sb("v1", [P, NT, NH, DK + 1])
    hmax = sb("hmax", [P, 2, NT])
    hsum = sb("hsum", [P, NT, NH])
    tgt2 = sb("tgt2", [P, NT, D])
    cN, xN = sb("cN", [P, 4, NT * D]), sb("xN", [P, 4, NT * D])
    zc, zy = sb("zc", [P, 4, NT * D]), sb("zy", [P, 4, NT * D])
    bn = sb("bn", [P, 2, 2, 4, 6])
    mv = sb("mv", [P, 3, 8])
    nmean = sb("nmean", [P, 2, 8])
    rstd = sb("rstd", [P, 2, 8])
    nwt = sb("nwt", [P, 2, 8])
    vps = sb("vps", [P, 2, 8])
    XT, FT = sb("XT", [P, 2, DC, N]), sb("FT", [P, 2, DC, N])
    Fall = sb("Fall", [P, B * DC * N])
    nmax = sb("nmax", [P, 2, NT])
    E = sb("E", [P, 2, NT * N])
    PT = sb("PT", [P, 2, NT * N])
    V1 = sb("V1", [P, 4, NT, H + 1])
    OA = sb("OA", [P, B, NT * (H + 1)])
    a5c = sb("a5c", [P, DC, H + 1])
    MT = sb("MT", [P, DC, U])
    prodQ = sb("prodQ", [P, DC, (H + 1) ** 2])
    prodK = sb("prodK", [P, DC, U * U])
    Q = sb("Q", [P, (H + 1) ** 2])
    K = sb("K", [P, U * U])
    rA = sb("rA", [P, TILES])
    hpre = sb("hpre", [P, TILES, H])
    ha = sb("ha", [P, TILES, H + 1])
    big = sb("big", [P, TILES * U * U])
    W5 = sb("W5", [P, TILES, H + 1])
    var = sb("var", [P, TILES])
    r3 = sb("r3", [P, TILES])
    t3 = sb("t3", [P, TILES])
    u = sb("u", [P, B, NT * U])
    uK = sb("uK", [P, TILES, U])
    w1s, b1s = sb("w1s", [P, DC]), sb("b1s", [P, DC])
    fc1s = sb("fc1s", [P, DC, H])
    g12 = sb("g12", [P, DC])
    cut = sb("cut", [P, TILES, CO])
    cutp = sb("cutp", [P, TILES, CO], BF16)
    stU = sb("stU", [P, B, 2, NT, SU], BF16)
    stC = sb("stC", [P, B, NT, SLOT], BF16)
    co = sb("co", [P, TILES, CO])
    Rt = sb("Rt", [P, DC, CO])
    Rcut = sb("Rcut", [P, DC, CO])
    Rp = sb("Rp", [P, DC, CO], BF16)
    stR = sb("stR", [P, DC, 2, SLOT], BF16)
    RT = sb("RT", [P, DC * P], BF16)
    sU = sb("sU", [P, 2, 2, NT, 2, SLOT], BF16)
    sT = sb("sT", [P, 2, 2 * NT * P], BF16)
    nm2 = sb("nm2", [P, 2, 2 * NT], BF16)
    nm2T = sb("nm2T", [4, 2, P], BF16)
    PT2 = sb("PT2", [P, 2, NT * N])
    OB = sb("OB", [P, B, NT * U])
    rB = sb("rB", [P, TILES])
    sC = sb("sC", [P, 2, NT, 2, SLOT], BF16)
    cT = sb("cT", [P, 2, NT * P], BF16)
    fin = sb("fin", [P, 4, DC * N])

    def c_(name, i=None, w=None):
        a, b = COLS[name]
        return par[:, a:b] if i is None else par[:, a + i:a + i + 1]

    par_in, q_in, k_in, v_in = sem("par_in"), sem("q_in"), sem("k_in"), sem("v_in")
    consts = sem("consts")
    q_mm, k_mm, v_mm = sem("q_mm"), sem("k_mm"), sem("v_mm")
    qT_ok, kT_ok, v1_ok = sem("qT_ok"), sem("kT_ok"), sem("v1_ok")
    s0_mm, max0_ok, exp0_ok = sem("s0_mm"), sem("max0_ok"), sem("exp0_ok")
    p0_mm, o0_mm = sem("p0_mm"), sem("o0_mm")
    pt0_ok = [sem("pt0_even"), sem("pt0_odd")]
    hsum_ok, tgt2_ok = sem("hsum_ok"), sem("tgt2_ok")
    c_in = [sem(f"c_in{j}") for j in range(4)]
    x_in = [sem(f"x_in{j}") for j in range(4)]
    y_ok, bn_ok = sem("y_ok"), sem("bn_ok")
    stat_ok, z_ok = sem("stat_ok"), sem("z_ok")
    xt_mm, yt_mm, XT_ok, FT_ok = sem("xt_mm"), sem("yt_mm"), sem("XT_ok"), sem("FT_ok")
    f_saved = [sem(f"f_saved{j}") for j in range(2)]
    s_mm, v_mm1, max_ok, exp_ok = sem("s_mm"), sem("v_mm1"), sem("max_ok"), sem("exp_ok")
    V1_ok, p_mm, PT_ok, o_mm, o_saved = sem("V1_ok"), sem("p_mm"), sem("PT_ok"), sem("o_mm"), sem("o_saved")
    alg = sem("alg")
    mean_mm, qk_mm, gelu_ok = sem("mean_mm"), sem("qk_mm"), sem("gelu_ok")
    r_mm, rt_ok, zero_ok = sem("r_mm"), sem("rt_ok"), sem("zero_ok")
    sU_ok, st_mm, sT_ok = sem("sU_ok"), sem("st_mm"), sem("sT_ok")
    s2_mm, max2_ok, m_mm, m_ok, s2m_mm = sem("s2_mm"), sem("max2_ok"), sem("m_mm"), sem("m_ok"), sem("s2m_mm")
    exp2_ok, o2_mm, o2_saved = sem("exp2_ok"), sem("o2_mm"), sem("o2_saved")
    sC_ok, ct_mm, cT_ok, f_mm, fin_ok = sem("sC_ok"), sem("ct_mm"), sem("cT_ok"), sem("f_mm"), sem("fin_ok")
    out_done = [sem(f"out_done{j}") for j in range(4)]

    x_d = x.rearrange("b (p t) d -> b p (t d)", t=NT)
    c_d = ctx.rearrange("b (p t) d -> b p (t d)", t=NT)
    out_d = out.rearrange("b p c n -> b p (c n)")

    def phase(eng, step, first, last, g0, g1):
        for i in range(first, 4 * g0):
            step(i, i % 4, i // 4)
        with eng.Fori(g0, g1) as g:
            for j in range(4):
                step(g * 4 + j, j, g)
        for i in range(4 * g1, last):
            step(i, i % 4, i // 4)

    def live(i, k):
        return not isinstance(i, int) or 0 <= i + k < B

    def later(i, k):
        return not isinstance(i, int) or i + k >= 0

    ALG = {}

    block = stack.enter_context(nc.Block())

    @block.sync
    def _(sp):
        sp.dma_start(par[:, :], params).then_inc(par_in, 16)
        for dst, src, arrived in ((x0T, x0t, q_in), (wqT, wqt, q_in), (c0T, c0t, k_in), (wkT, wkt, k_in),
                                  (wvT, wvt, v_in)):
            sp.dma_start(dst[:, :, :], src).then_inc(arrived, 16)

        def step(i, j, g):
            if live(i, 6):
                slot = (j + 6) % 4
                if later(i, 2):
                    sp.wait_ge(z_ok, 4 * (i + 3))
                sp.dma_start(cN[:, slot, :], c_d[i + 6, :, :]).then_inc(c_in[slot], 16)
                sp.dma_start(xN[:, slot, :], x_d[i + 6, :, :]).then_inc(x_in[slot], 16)
            if live(i, 1):
                sp.wait_ge(FT_ok, 2 * (i + 2))
                sp.dma_start(Fall[:, bass.ds((i + 1) * (DC * N), DC * N)],
                             FT[:, (j + 1) % 2, :, :].rearrange("p c n -> p (c n)"))\
                    .then_inc(f_saved[(j + 1) % 2], 16)

        phase(sp, step, -6, B, 1, 6)
        for s in f_saved:
            sp.wait_ge(s, 16 * (B // 2))

        def store(g):
            for j in range(4):
                sp.wait_ge(fin_ok, g * 4 + j + 1)
                sp.dma_start(out_d[g * 4 + j, :, :], fin[:, j, :]).then_inc(out_done[j], 16)

        with sp.Fori(0, B // 4) as g:
            store(g)
        for s in out_done:
            sp.wait_ge(s, 16 * (B // 4))

    @block.gpsimd
    def _(pool):
        pool.memset(ident[:, :], 0.0).then_inc(consts, 1)
        pool.memset(identb[:, :], 0.0).then_inc(consts, 1)
        pool.memset(sel[:, :], 0.0).then_inc(consts, 1)
        pool.wait_ge(consts, 3)
        pool.affine_select(out=ident[:, :], in_=ident[:, :], compare_op=ALU.not_equal, fill=1.0, base=0,
                           pattern=[[-1, P]], channel_multiplier=1).then_inc(consts, 1)
        pool.affine_select(out=identb[:, :], in_=identb[:, :], compare_op=ALU.not_equal, fill=1.0, base=0,
                           pattern=[[-1, P]], channel_multiplier=1).then_inc(consts, 1)
        pool.affine_select(out=sel[:, :], in_=sel[:, :], compare_op=ALU.not_equal, fill=1.0, base=0,
                           pattern=[[-1, 4], [0, P]], channel_multiplier=1).then_inc(consts, 1)
        pool.memset(meanw[:, :], 1.0 / D).then_inc(consts, 1)
        pool.memset(scalew[:, :], SCALE1).then_inc(consts, 1)
        pool.memset(v1[:, :, :, DK:DK + 1], 1.0).then_inc(consts, 1)
        pool.memset(V1[:, :, :, H:H + 1], 1.0).then_inc(consts, 1)
        pool.memset(sU[:, :, :, :, :, :], 0.0).then_inc(zero_ok, 1)
        pool.memset(stC[:, :, :, :], 0.0).then_inc(zero_ok, 1)
        pool.memset(stR[:, :, :, :], 0.0).then_inc(zero_ok, 1)
        pool.memset(ha[:, :, H:H + 1], 1.0).then_inc(zero_ok, 1)
        pool.memset(u[:, :, :].rearrange("p b (t u) -> p (b t) u", u=U)[:, :, U - 1:U], 1.0).then_inc(zero_ok, 1)
        pool.memset(co[:, :, CO - 1:CO], 1.0).then_inc(zero_ok, 1)

        def step(i, j, g):
            zslot, pair, m = (j + 3) % 4, ((j + 3) // 2) % 2, (j + 3) % 2
            if live(i, 3):
                pool.wait_ge(stat_ok, (2 * g + (j + 3) // 2 + 1) * NCHAIN)
                if later(i, -1):
                    pool.wait_ge(yt_mm, i)
            if live(i, 5):
                slot = (j + 5) % 4
                use = g * 4 + j + 5 - slot
                if isinstance(i, int) and i + 5 == 0:
                    pool.wait_ge(tgt2_ok, NT)
                pool.wait_ge(x_in[slot], use * 4 + 16)
                pool.tensor_tensor(xN[:, slot, :], xN[:, slot, :], tgt2[:, :, :].rearrange("p t d -> p (t d)"),
                                   ALU.add).then_inc(y_ok, 1)
            if live(i, 3):
                for t in range(2 * NT):
                    src, dst = ((cN, zc) if t < NT else (xN, zy))
                    cols = slice((t % NT) * D, (t % NT + 1) * D)
                    k = m * 4 + t
                    pool.tensor_scalar(dst[:, zslot, cols], src[:, zslot, cols], nmean[:, pair, k:k + 1],
                                       rstd[:, pair, k:k + 1], ALU.add, ALU.mult).then_inc(z_ok, 1)

        phase(pool, step, -5, B, 1, 6)

    @block.vector
    def _(dve):
        count = [0]

        def link(ins, name=None):
            ins.then_inc(alg, 1)
            count[0] += 1
            dve.wait_ge(alg, count[0])
            if name:
                ALG[name] = count[0]

        def cuts(v, left, part, slots, order):
            for k in range(3):
                link(dve.tensor_copy(part, v))
                if k < 2:
                    link(dve.tensor_tensor(left, v, part, ALU.subtract))
                for s, o in enumerate(order):
                    if o == k:
                        link(dve.tensor_copy(slots(s), part))
                v = left

        dve.wait_ge(par_in, 16)
        a5 = c_("a5").rearrange("p (c k) -> p c k", c=DC)
        link(dve.tensor_scalar(w1s[:, :], c_("w1"), SCALE1, None, ALU.mult))
        link(dve.tensor_scalar(b1s[:, :], c_("b1"), SCALE1, None, ALU.mult))
        link(dve.tensor_scalar(fc1s[:, :, :], c_("fc1").rearrange("p (c k) -> p c k", c=DC), 1.0 / SCALE1, None,
                               ALU.mult), "scaled")
        dve.wait_ge(mean_mm, 1)
        link(dve.tensor_tensor(a5c[:, :, :], a5, bank[6][:, 0:H + 1].unsqueeze(1).to_broadcast([P, DC, H + 1]),
                               ALU.subtract))
        for c in range(DC):
            link(dve.tensor_scalar(MT[:, c, 0:H + 1], a5c[:, c, :], c_("w3", c), None, ALU.mult))
            link(dve.tensor_copy(MT[:, c, U - 1:U], c_("b3", c)))
        for dst, src, n in ((prodQ, a5c, H + 1), (prodK, MT, U)):
            for c in range(DC):
                link(dve.tensor_tensor(dst[:, c, :].rearrange("p (i j) -> p i j", i=n),
                                       src[:, c, :].unsqueeze(2).to_broadcast([P, n, n]),
                                       src[:, c, :].unsqueeze(1).to_broadcast([P, n, n]), ALU.mult), "prods")
        link(dve.tensor_tensor(g12[:, :], c_("g1"), c_("g2"), ALU.mult))
        for c in range(DC):
            link(dve.tensor_scalar(Rt[:, c, 0:H], a5[:, c, 0:H], c_("g2", c), None, ALU.mult))
            link(dve.tensor_scalar(Rt[:, c, H:CO], MT[:, c, :], g12[:, c:c + 1], None, ALU.mult))
            link(dve.scalar_tensor_tensor(Rt[:, c, CO - 1:CO], a5[:, c, H:H + 1], c_("g2", c), Rt[:, c, CO - 1:CO],
                                          ALU.mult, ALU.add))
        dve.wait_ge(zero_ok, 6)
        for m in range(2):
            cuts(Rt[:, :, :], Rcut[:, :, :], Rp[:, :, :], lambda s: stR[:, :, m, s * CO:(s + 1) * CO], PARTS_L)
        ALG["stR"] = count[0]
        dve.wait_ge(qk_mm, 1)
        link(dve.tensor_copy(Q[:, :], bank[7][:, 0:(H + 1) ** 2]))
        link(dve.tensor_copy(K[:, :], bank[7][:, 64:64 + U * U]))
        dve.wait_ge(r_mm, 1)
        link(dve.tensor_copy(RT[:, :], bank[5][:, 0:DC * P // 2].bitcast(BF16)), "RT")

        dve.wait_ge(k_mm, 1)
        for e, m in enumerate(("even", "odd")):
            dve.tensor_scalar(kTm[:, e, :, :], tiles(bank[1]), c_(m), None, ALU.mult).then_inc(kT_ok, 1)
        for h in range(NH + 1):
            if h < NH:
                dve.wait_ge(s0_mm, h + 1)
                if h >= 2:
                    dve.wait_ge(exp0_ok, 2 * (h - 1))
                dve.tensor_reduce(hmax[:, h % 2, :], tiles(bank[3 + h % 2]), AX.X, ALU.max, negate=True)\
                    .then_inc(max0_ok, 1)
            if h >= 1 and (h - 1) % 2 == 1:
                dve.wait_ge(p0_mm, h)
                if h >= 3:
                    dve.wait_ge(o0_mm, h - 2)
                dve.tensor_copy(PT[:, (h - 1) % 2, :], bank[5 + (h - 1) % 2][:, :]).then_inc(pt0_ok[1], 1)
        dve.wait_ge(o0_mm, NH)
        for t in range(NT):
            o = bank[t][:, 0:NH * (DK + 1)].rearrange("p (h k) -> p h k", h=NH)
            dve.reciprocal(hsum[:, t, :].unsqueeze(2), o[:, :, DK:DK + 1]).then_inc(hsum_ok, 1)
        for t in range(NT):
            o = bank[t][:, 0:NH * (DK + 1)].rearrange("p (h k) -> p h k", h=NH)
            dve.wait_ge(hsum_ok, t + 1)
            dve.tensor_tensor(tgt2[:, t, :].rearrange("p (h k) -> p h k", h=NH), o[:, :, 0:DK],
                              hsum[:, t, :].unsqueeze(2).to_broadcast([P, NH, DK]), ALU.mult).then_inc(tgt2_ok, 1)

        def rsqrt(v, y, t, chain):
            chain(dve.tensor_scalar(y.bitcast(I32), v.bitcast(I32), 1, None, ALU.logical_shift_right))
            chain(dve.tensor_scalar(y.bitcast(I32), y.bitcast(I32), -1.0, RSQRT_SEED, ALU.mult, ALU.add))
            for _ in range(NEWTON):
                chain(dve.tensor_tensor(t, y, y, ALU.mult))
                chain(dve.scalar_tensor_tensor(t, t, -0.5, v, ALU.mult, ALU.mult))
                chain(dve.scalar_tensor_tensor(y, t, 1.5, y, ALU.add, ALU.mult))

        def step(i, j, g):
            if live(i, 4):
                slot, pr, m = j, (j // 2) % 2, j % 2
                dve.wait_ge(c_in[slot], g * 16 + 32)
                dve.wait_ge(y_ok, i + 5)
                for t in range(2 * NT):
                    src = cN if t < NT else xN
                    dve.bn_stats(bn[:, pr, m, t, :], src[:, slot, (t % NT) * D:(t % NT + 1) * D]).then_inc(bn_ok, 1)
                if m == 1:
                    done = [(2 * g + (j + 4) // 2) * NCHAIN]

                    def inc(ins):
                        ins.then_inc(stat_ok, 1)
                        done[0] = done[0] + 1

                    def chain(ins):
                        inc(ins)
                        dve.wait_ge(stat_ok, done[0])

                    half = bn[:, pr, :, :, :].rearrange("p m t s -> p (m t) s")
                    total, apart, squares = (mv[:, k, :].unsqueeze(2) for k in range(3))
                    if later(i, 0):
                        dve.wait_ge(z_ok, 4 * (i + 1))
                    dve.wait_ge(bn_ok, 4 * (i + 5))
                    inc(dve.tensor_tensor(apart, half[:, :, 1:2], half[:, :, 4:5], ALU.subtract))
                    inc(dve.tensor_tensor(total, half[:, :, 1:2], half[:, :, 4:5], ALU.add))
                    chain(dve.tensor_tensor(squares, half[:, :, 2:3], half[:, :, 5:6], ALU.add))
                    inc(dve.tensor_scalar(nmean[:, pr, :], mv[:, 0, :], -0.5, None, ALU.mult))
                    chain(dve.tensor_tensor(apart, apart, apart, ALU.mult))
                    chain(dve.scalar_tensor_tensor(vps[:, pr, :], mv[:, 1, :], D / 4.0, mv[:, 2, :], ALU.mult, ALU.add))
                    chain(dve.tensor_scalar(vps[:, pr, :], vps[:, pr, :], 1.0 / D, EPS, ALU.mult, ALU.add))
                    rsqrt(vps[:, pr, :], rstd[:, pr, :], nwt[:, pr, :], chain)
            if live(i, 0):
                dve.wait_ge(s_mm, i + 1)
                if later(i, -2):
                    dve.wait_ge(exp_ok, 2 * i - 2)
                dve.tensor_reduce(nmax[:, j % 2, :], tiles(bank[2 + j % 2]), AX.X, ALU.max, negate=True)\
                    .then_inc(max_ok, 1)
                dve.wait_ge(v_mm1, i + 1)
                if later(i, -4):
                    dve.wait_ge(o_mm, i - 3)
                dve.tensor_copy(V1[:, j, :, 0:H], bank[6][:, 0:NT * H].rearrange("p (t h) -> p t h", t=NT))\
                    .then_inc(V1_ok, 1)
            if live(i, -2):
                dve.wait_ge(o_mm, i - 1)
                dve.tensor_copy(OA[:, bass.ds(i - 2, 1), :], bank[7][:, 0:NT * (H + 1)].unsqueeze(1)).then_inc(o_saved, 1)

        phase(dve, step, -4, B + 2, 1, 7)

        def spread(ap, w):
            return ap.unsqueeze(2).to_broadcast([P, TILES, w])

        def quadratic(dst, v, m, n):
            w = big[:, 0:TILES * n * n].rearrange("p (t j i) -> p t j i", t=TILES, j=n)
            link(dve.tensor_tensor(w, v.unsqueeze(2).to_broadcast([P, TILES, n, n]),
                                   m.rearrange("p (j i) -> p j i", j=n).unsqueeze(1).to_broadcast([P, TILES, n, n]),
                                   ALU.mult))
            link(dve.tensor_reduce(dst, w, AX.X, ALU.add))

        dve.wait_ge(o_saved, B)
        oa = OA[:, :, :].rearrange("p b (t k) -> p (b t) k", t=NT)
        ut = u[:, :, :].rearrange("p b (t k) -> p (b t) k", t=NT)
        link(dve.reciprocal(rA[:, :].unsqueeze(2), oa[:, :, H:H + 1]))
        link(dve.tensor_tensor(hpre[:, :, :], oa[:, :, 0:H], spread(rA[:, :], H), ALU.mult))
        link(dve.tensor_tensor(hpre[:, :, :], hpre[:, :, :], c_("fc1b").unsqueeze(1).to_broadcast([P, TILES, H]),
                               ALU.add), "hpre")
        dve.wait_ge(gelu_ok, 1)
        quadratic(W5[:, :, :], ha[:, :, :], Q[:, :], H + 1)
        link(dve.tensor_tensor(W5[:, :, :], W5[:, :, :], ha[:, :, :], ALU.mult))
        link(dve.tensor_reduce(var[:, :], W5[:, :, :], AX.X, ALU.add))
        link(dve.tensor_scalar(var[:, :], var[:, :], EPS, None, ALU.add))
        rsqrt(var[:, :], r3[:, :], t3[:, :], link)
        link(dve.tensor_tensor(ut[:, :, 0:H + 1], ha[:, :, :], spread(r3[:, :], H + 1), ALU.mult), "u")
        quadratic(uK[:, :, :], ut, K[:, :], U)
        for side, v, order in ((0, uK[:, :, :], PARTS_L), (1, ut, PARTS_R)):
            cuts(v, cut[:, :, 0:U], cutp[:, :, 0:U],
                 lambda s: stU[:, :, side, :, s * U:(s + 1) * U], order)
        ALG["stU"] = count[0]

        def pair(p, r, first=False, ahead=True, behind=True):
            if ahead:
                dve.wait_ge(st_mm, p + 2)
                if not first:
                    dve.wait_ge(s2_mm, p * 2)
                dve.tensor_copy(sT[:, 1 - r, :], bank[4][:, 0:NT * P].bitcast(BF16)).then_inc(sT_ok, 1)
                if not first:
                    dve.wait_ge(m_mm, p)
                for m in range(2):
                    dve.wait_ge(s2_mm, p * 2 + (m + 3))
                    dve.tensor_reduce(nm2[:, 1 - r, NT * m:NT * (m + 1)], tiles(bank[2 * (1 - r) + m]), AX.X, ALU.max,
                                      negate=True).then_inc(max2_ok, 1)
            if behind:
                dve.wait_ge(o2_mm, p)
                dve.tensor_copy(OB[:, bass.ds(p * 2 - 2, 2), :],
                                bank[6][:, 0:2 * NT * U].rearrange("p (m k) -> p m k", m=2)).then_inc(o2_saved, 1)

        pair(-1, 1, first=True, behind=False)
        pair(0, 0, first=True, behind=False)
        pair(1, 1)
        with dve.Fori(1, B // 4 - 1) as g:
            pair(g * 2, 0)
            pair(g * 2 + 1, 1)
        pair(B // 2 - 2, 0)
        pair(B // 2 - 1, 1, ahead=False)
        pair(B // 2, 0, ahead=False)

        dve.wait_ge(o2_saved, B // 2)
        ob = OB[:, :, :].rearrange("p b (t k) -> p (b t) k", t=NT)
        link(dve.reciprocal(rB[:, :].unsqueeze(2), ob[:, :, U - 1:U]))
        link(dve.tensor_tensor(co[:, :, H:CO - 1], ob[:, :, 0:H + 1], spread(rB[:, :], H + 1), ALU.mult))
        link(dve.tensor_copy(co[:, :, 0:H], ha[:, :, 0:H]))
        cuts(co[:, :, :].rearrange("p (b t) k -> p b t k", t=NT), cut[:, :, :].rearrange("p (b t) k -> p b t k", t=NT),
             cutp[:, :, :].rearrange("p (b t) k -> p b t k", t=NT), lambda s: stC[:, :, :, s * CO:(s + 1) * CO], PARTS_R)
        ALG["stC"] = count[0]

        def results(g, first=False):
            for j in range(4):
                dve.wait_ge(f_mm, g * 4 + (j + 1))
                if not first:
                    dve.wait_ge(out_done[j], g * 16)
                dve.tensor_tensor(fin[:, j, :], bank[j][:, :],
                                  Fall[:, bass.ds(g * (4 * DC * N) + j * DC * N, DC * N)], ALU.add).then_inc(fin_ok, 1)

        results(0, first=True)
        with dve.Fori(1, B // 4) as g:
            results(g)

    @block.scalar
    def _(act):
        act.wait_ge(q_mm, 1)
        act.activation(qT[:, :, :], tiles(bank[0]), ACT.Copy, scale=float(DK) ** -0.5).then_inc(qT_ok, 1)
        act.wait_ge(v_mm, 1)
        act.wait_ge(consts, 9)
        for t in range(NT):
            act.activation(v1[:, t, :, 0:DK], bank[2][:, t * D:(t + 1) * D].rearrange("p (h k) -> p h k", h=NH),
                           ACT.Copy).then_inc(v1_ok, 1)
        for h in range(NH + 1):
            if h < NH:
                act.wait_ge(max0_ok, h + 1)
                if h >= 2:
                    act.wait_ge(p0_mm, h - 1)
                for t in range(NT):
                    act.activation(E[:, h % 2, t * N:(t + 1) * N], bank[3 + h % 2][:, t * N:(t + 1) * N], ACT.Exp,
                                   bias=hmax[:, h % 2, t:t + 1]).then_inc(exp0_ok, 1)
            if h >= 1 and (h - 1) % 2 == 0:
                act.wait_ge(p0_mm, h)
                if h >= 3:
                    act.wait_ge(o0_mm, h - 2)
                act.activation(PT[:, (h - 1) % 2, :], bank[5 + (h - 1) % 2][:, :], ACT.Copy).then_inc(pt0_ok[0], 1)

        def step(i, j, g):
            n = (j + 1) % 2
            if live(i, 1):
                act.wait_ge(yt_mm, i + 2)
                if later(i, -1):
                    act.wait_ge(s_mm, i)
                    act.wait_ge(f_saved[n], (g * 4 + j + 1 - n) * 8)
                for c in range(DC):
                    act.activation(FT[:, n, c, :], bank[1][:, c * N:(c + 1) * N], ACT.Identity,
                                   bias=c_("b2", c), scale=c_("w2", c)).then_inc(FT_ok, 1)
                if later(i, -1):
                    act.wait_ge(v_mm1, i)
                for c in range(DC):
                    act.activation(XT[:, n, c, :], bank[0][:, c * N:(c + 1) * N], ACT.Identity,
                                   bias=b1s[:, c:c + 1], scale=w1s[:, c:c + 1]).then_inc(XT_ok, 1)
            if live(i, 0):
                act.wait_ge(max_ok, i + 1)
                if later(i, -2):
                    act.wait_ge(p_mm, i - 1)
                for t in range(NT):
                    act.activation(E[:, j % 2, t * N:(t + 1) * N], bank[2 + j % 2][:, t * N:(t + 1) * N], ACT.Exp,
                                   bias=nmax[:, j % 2, t:t + 1]).then_inc(exp_ok, 1)
            if live(i, -1):
                act.wait_ge(p_mm, i)
                if later(i, -3):
                    act.wait_ge(o_mm, i - 2)
                act.activation(PT[:, n, :], bank[4 + n][:, :], ACT.Copy).then_inc(PT_ok, 1)

        phase(act, step, -1, B + 1, 1, 7)

        act.wait_ge(alg, ALG["hpre"])
        act.activation(ha[:, :, 0:H], hpre[:, :, :], ACT.Gelu).then_inc(gelu_ok, 1)

        def copy(p, r):
            for m in range(2):
                act.activation(sU[:, r, :, :, m, 0:SU], stU[:, bass.ds(p * 2 + m, 1), :, :, :],
                               ACT.Copy).then_inc(sU_ok, 1)

        def pair(p, r, first=False, ahead=True):
            if ahead:
                act.wait_ge(st_mm, p + 1)
                copy(p + 2, r)
            act.wait_ge(m_mm, p + 1)
            if not first:
                act.wait_ge(s2m_mm, p * 2 - 2)
            act.activation(nm2T[:, r, :], bank[5][0:4, 0:P // 2].bitcast(BF16), ACT.Copy).then_inc(m_ok, 1)
            for m in range(2):
                act.wait_ge(s2m_mm, p * 2 + (m + 1))
                if not first:
                    act.wait_ge(o2_mm, p)
                act.activation(PT2[:, m, :], bank[2 * r + m][:, :], ACT.Exp).then_inc(exp2_ok, 1)

        act.wait_ge(zero_ok, 6)
        act.wait_ge(alg, ALG["stU"])
        copy(0, 0)
        copy(1, 1)
        pair(0, 0, first=True)
        pair(1, 1)
        with act.Fori(1, B // 4 - 1) as g:
            pair(g * 2, 0)
            pair(g * 2 + 1, 1)
        pair(B // 2 - 2, 0, ahead=False)
        pair(B // 2 - 1, 1, ahead=False)

        def copy3(p, r):
            act.activation(sC[:, r, :, :, :], stC[:, bass.ds(p * 2, 2), :, :].rearrange("p b t r -> p t b r"),
                           ACT.Copy).then_inc(sC_ok, 1)

        def pair3(p, r, first=False, ahead=True):
            act.wait_ge(ct_mm, p + 1)
            if not first:
                act.wait_ge(f_mm, p * 2 - 2)
            act.activation(cT[:, r, :], bank[4 + r][:, 0:NT * P // 2].bitcast(BF16), ACT.Copy).then_inc(cT_ok, 1)
            if ahead:
                copy3(p + 2, r)

        act.wait_ge(alg, ALG["stC"])
        copy3(0, 0)
        copy3(1, 1)
        pair3(0, 0, first=True)
        pair3(1, 1, first=True)
        with act.Fori(1, B // 4 - 1) as g:
            pair3(g * 2, 0)
            pair3(g * 2 + 1, 1)
        pair3(B // 2 - 2, 0, ahead=False)
        pair3(B // 2 - 1, 1, ahead=False)

    @block.tensor
    def _(pe):
        pe.wait_ge(par_in, 16)
        pe.wait_ge(consts, 8)
        a5 = c_("a5").rearrange("p (c k) -> p c k", c=DC)
        for c in range(DC):
            last = pe.matmul(bank[6][:, 0:H + 1], meanw[:, :], a5[:, c, :], start=c == 0, stop=c == DC - 1)
        last.then_inc(mean_mm, 1)
        for arrived, n, w, src, b, done in ((q_in, 32, wqT, x0T, 0, q_mm), (k_in, 32, wkT, c0T, 1, k_mm)):
            pe.wait_ge(arrived, n)
            for o in range(2):
                for c in range(DC):
                    last = pe.matmul(bank[b][:, o * N:(o + 1) * N], w[:, c, o * P:(o + 1) * P], src[:, c, :],
                                     start=c == 0, stop=c == DC - 1)
            last.then_inc(done, 1)
        pe.wait_ge(v_in, 16)
        for t in range(NT):
            for c in range(DC):
                last = pe.matmul(bank[2][:, t * D:(t + 1) * D], c0T[:, c, t * P:(t + 1) * P], wvT[:, c, :],
                                 start=c == 0, stop=c == DC - 1)
        last.then_inc(v_mm, 1)
        pe.wait_ge(alg, ALG["prods"])
        for dst, w, src, n in ((0, meanw, prodQ, (H + 1) ** 2), (64, scalew, prodK, U * U)):
            for c in range(DC):
                last = pe.matmul(bank[7][:, dst:dst + n], w[:, :], src[:, c, :], start=c == 0, stop=c == DC - 1)
        last.then_inc(qk_mm, 1)
        pe.wait_ge(alg, ALG["stR"])
        for c in range(DC):
            last = pe.transpose(bank[5][:, c * P // 2:(c + 1) * P // 2].bitcast(BF16),
                                stR[:, c, :, :].rearrange("p m r -> p (m r)"), identb[:, :])
        last.then_inc(r_mm, 1)

        pe.wait_ge(qT_ok, 1)
        pe.wait_ge(kT_ok, 2)
        for h in range(NH + 2):
            if h < NH:
                o, q, e = h // 8, 32 * ((h % 8) // 2), h % 2
                if h >= 2:
                    pe.wait_ge(exp0_ok, 2 * (h - 1))
                for t in range(NT):
                    last = pe.matmul(bank[3 + h % 2][:, t * N:(t + 1) * N], qT[q:q + 32, o, t * P:(t + 1) * P],
                                     kTm[q:q + 32, e, o, :], start=True, stop=True)
                last.then_inc(s0_mm, 1)
            if 1 <= h <= NH:
                if h == 1:
                    pe.wait_ge(alg, ALG["RT"])
                pe.wait_ge(exp0_ok, 2 * h)
                if h >= 3:
                    pe.wait_ge(pt0_ok[(h - 1) % 2], (h - 1) // 2)
                n = (h - 1) % 2
                for k in range(NT):
                    for t in range(NT):
                        last = pe.transpose(bank[5 + n][:, k * N + t * P:k * N + (t + 1) * P],
                                            E[:, n, t * N + k * P:t * N + (k + 1) * P], ident[:, :])
                last.then_inc(p0_mm, 1)
            if h >= 2:
                if h == 2:
                    pe.wait_ge(v1_ok, 2)
                pe.wait_ge(pt0_ok[h % 2], h // 2)
                for t in range(NT):
                    for k in range(NT):
                        last = pe.matmul(bank[t][:, (h - 2) * (DK + 1):(h - 1) * (DK + 1)],
                                         PT[:, h % 2, k * N + t * P:k * N + (t + 1) * P], v1[:, k, h - 2, :],
                                         start=k == 0, stop=k == NT - 1)
                last.then_inc(o0_mm, 1)

        fc1 = fc1s
        def step(i, j, g):
            n = (j + 1) % 2
            if live(i, 1):
                pe.wait_ge(z_ok, 4 * (i + 2))
                if later(i, 0):
                    pe.wait_ge(XT_ok, 2 * (i + 1))
                    pe.wait_ge(FT_ok, 2 * (i + 1))
                for b, z, done in ((0, zc, xt_mm), (1, zy, yt_mm)):
                    for c in range(DC):
                        for t in range(NT):
                            last = pe.transpose(bank[b][:, c * N + t * P:c * N + (t + 1) * P],
                                                z[:, (j + 1) % 4, t * D + c * P:t * D + (c + 1) * P], ident[:, :])
                    last.then_inc(done, 1)
            if live(i, 0):
                pe.wait_ge(FT_ok, 2 * (i + 1))
                pe.wait_ge(XT_ok, 2 * (i + 1))
                if later(i, -2):
                    pe.wait_ge(exp_ok, 2 * i - 2)
                for t in range(NT):
                    for c in range(DC):
                        last = pe.matmul(bank[2 + j % 2][:, t * N:(t + 1) * N], FT[:, j % 2, c, t * P:(t + 1) * P],
                                         XT[:, j % 2, c, :], start=c == 0, stop=c == DC - 1)
                last.then_inc(s_mm, 1)
                if later(i, -1):
                    pe.wait_ge(V1_ok, i)
                for t in range(NT):
                    for c in range(DC):
                        last = pe.matmul(bank[6][:, t * H:(t + 1) * H], XT[:, j % 2, c, t * P:(t + 1) * P],
                                         fc1[:, c, :], start=c == 0, stop=c == DC - 1)
                last.then_inc(v_mm1, 1)
            if live(i, -1):
                pe.wait_ge(exp_ok, 2 * i)
                if later(i, -3):
                    pe.wait_ge(PT_ok, i - 2)
                for k in range(NT):
                    for t in range(NT):
                        last = pe.transpose(bank[4 + n][:, k * N + t * P:k * N + (t + 1) * P],
                                            E[:, n, t * N + k * P:t * N + (k + 1) * P], ident[:, :])
                last.then_inc(p_mm, 1)
            if live(i, -2):
                pe.wait_ge(PT_ok, i - 1)
                pe.wait_ge(V1_ok, i - 1)
                if later(i, -3):
                    pe.wait_ge(o_saved, i - 2)
                for t in range(NT):
                    for k in range(NT):
                        last = pe.matmul(bank[7][:, t * (H + 1):(t + 1) * (H + 1)],
                                         PT[:, j % 2, k * N + t * P:k * N + (t + 1) * P], V1[:, (j + 2) % 4, k, :],
                                         start=k == 0, stop=k == NT - 1)
                last.then_inc(o_mm, 1)

        phase(pe, step, -1, B + 2, 1, 7)

        def pair(p, r, first=False, ahead=True, now=True, behind=True):
            if ahead:
                pe.wait_ge(sU_ok, p * 2 + 4)
                if not first:
                    pe.wait_ge(sT_ok, p + 1)
                for side in range(2):
                    for t in range(NT):
                        k = (side * NT + t) * P // 2
                        last = pe.transpose(bank[4][:, k:k + P // 2].bitcast(BF16),
                                            sU[:, 1 - r, side, t, :, :].rearrange("p m r -> p (m r)"), identb[:, :])
                last.then_inc(st_mm, 1)
                pe.wait_ge(sT_ok, p + 2)
                if not first:
                    pe.wait_ge(exp2_ok, p * 2)
                for m in range(2):
                    rows = slice(SLOT * m, SLOT * m + SU)
                    for k in range(NT):
                        last = pe.matmul(bank[2 * (1 - r) + m][:, k * N:(k + 1) * N],
                                         sT[rows, 1 - r, k * P:(k + 1) * P], sT[rows, 1 - r, NT * P:2 * NT * P],
                                         start=k == 0, stop=True, skip_group_check=True)
                    last.then_inc(s2_mm, 1)
            if now:
                pe.wait_ge(max2_ok, p * 2 + 2)
                if not first:
                    pe.wait_ge(m_ok, p)
                pe.transpose(bank[5][0:4, 0:P // 2].bitcast(BF16), nm2[:, r, :], identb[:, :]).then_inc(m_mm, 1)
            if behind:
                pe.wait_ge(exp2_ok, p * 2)
                if not isinstance(p, int) or p >= 2:
                    pe.wait_ge(o2_saved, p - 1)
                for m in range(2):
                    for t in range(NT):
                        for k in range(NT):
                            last = pe.matmul(bank[6][:, (m * NT + t) * U:(m * NT + t + 1) * U],
                                             PT2[:, m, k * N + t * P:k * N + (t + 1) * P],
                                             u[:, bass.ds(p * 2 - 2 + m, 1), k * U:(k + 1) * U]
                                             .rearrange("p b k -> p (b k)"), start=k == 0, stop=k == NT - 1)
                last.then_inc(o2_mm, 1)
            if now:
                pe.wait_ge(m_ok, p + 1)
                for m in range(2):
                    for t in range(NT):
                        last = pe.matmul(tiles(bank[2 * r + m])[:, :, t * P:(t + 1) * P],
                                         sel[:, (m * NT + t) * P:(m * NT + t + 1) * P],
                                         nm2T[:, r, :].unsqueeze(1).to_broadcast([4, NT, P]), start=False, stop=True,
                                         skip_group_check=True)
                    last.then_inc(s2m_mm, 1)

        pair(-1, 1, first=True, now=False, behind=False)
        pair(0, 0, first=True, behind=False)
        pair(1, 1)
        with pe.Fori(1, B // 4 - 1) as g:
            pair(g * 2, 0)
            pair(g * 2 + 1, 1)
        pair(B // 2 - 2, 0)
        pair(B // 2 - 1, 1, ahead=False)
        pair(B // 2, 0, ahead=False, now=False)

        def pair3(p, r, first=False, ahead=True, now=True):
            if ahead:
                pe.wait_ge(sC_ok, p + 2)
                if not first:
                    pe.wait_ge(cT_ok, p)
                for t in range(NT):
                    last = pe.transpose(bank[5 - r][:, t * P // 2:(t + 1) * P // 2].bitcast(BF16),
                                        sC[:, 1 - r, t, :, :].rearrange("p m r -> p (m r)"), identb[:, :])
                last.then_inc(ct_mm, 1)
            if now:
                pe.wait_ge(cT_ok, p + 1)
                for m in range(2):
                    rows = slice(SLOT * m, SLOT * m + SC)
                    if not isinstance(p, int) or p >= 2:
                        pe.wait_ge(fin_ok, p * 2 + m - 3)
                    for c in range(DC):
                        last = pe.matmul(bank[2 * r + m][:, c * N:(c + 1) * N], RT[rows, c * P:(c + 1) * P],
                                         cT[rows, r, :], start=True, stop=True)
                    last.then_inc(f_mm, 1)

        pair3(-1, 1, first=True, now=False)
        pair3(0, 0, first=True)
        pair3(1, 1)
        with pe.Fori(1, B // 4 - 1) as g:
            pair3(g * 2, 0)
            pair3(g * 2 + 1, 1)
        pair3(B // 2 - 2, 0)
        pair3(B // 2 - 1, 1, ahead=False)

    stack.close()


def kernel(**inputs):
    import numpy as np
    import concourse.bacc as bacc
    from concourse.bass_utils import run_bass_kernel_spmd

    a = {k: np.asarray(v) for k, v in inputs.items()}

    def columns(v):
        return v.reshape(DC, P, -1).transpose(1, 0, 2).reshape(P, -1)

    def by_feature(m):
        return m.T.reshape(DC, P, -1).transpose(1, 0, 2)

    def tokens(m):
        return m.reshape(P, NT, D).transpose(1, 0, 2).reshape(N, D)

    even = (np.arange(P) // DK % 2 == 0).astype(np.float32)
    pieces = {
        "w1": columns(a["L1_xattn_norm1_w"]), "b1": columns(a["L1_xattn_norm1_b"]),
        "w2": columns(a["L1_xattn_norm2_w"]), "b2": columns(a["L1_xattn_norm2_b"]),
        "w3": columns(a["L1_xattn_norm3_w"]), "b3": columns(a["L1_xattn_norm3_b"]),
        "g1": columns(a["L1_xattn_gamma1"]), "g2": columns(a["L1_xattn_gamma2"]),
        "even": even[:, None], "odd": np.logical_not(even)[:, None].astype(np.float32),
        "fc1b": np.broadcast_to(a["L1_xattn_fc1_b"][None, :], (P, H)),
        "a5": columns(np.concatenate([a["L1_xattn_fc2_w"], a["L1_xattn_fc2_b"][:, None]], axis=1)),
        "fc1": columns(a["L1_xattn_fc1_w"].T),
    }
    arrays = {
        "x": a["x"], "ctx": a["ctx_1024"],
        "x0t": by_feature(tokens(a["x"][0])), "c0t": by_feature(tokens(a["ctx_1024"][0])),
        "wqt": by_feature(a["L0_xattn_Wq"]), "wkt": by_feature(a["L0_xattn_Wk"]), "wvt": by_feature(a["L0_xattn_Wv"]),
        "params": np.concatenate([pieces[k] for k in COLS], axis=1),
    }
    arrays = {k: np.ascontiguousarray(v) for k, v in arrays.items()}
    nc = bacc.Bacc("TRN2", target_bir_lowering=False, num_devices=1)
    args = [nc.dram_tensor(k, v.shape, mybir.dt.from_np(v.dtype), kind="ExternalInput").ap() for k, v in arrays.items()]
    args.append(nc.dram_tensor("out", (B, P, DC, N), F32, kind="ExternalOutput").ap())
    build(nc, *args)
    got = run_bass_kernel_spmd(nc, [arrays], core_ids=[0]).results[0]["out"]
    return got.reshape(B, P, DC, NT, P).transpose(0, 4, 3, 2, 1).reshape(B, N, D)
```

```python
from contextlib import ExitStack

import concourse.bass as bass
from concourse import mybir

F32 = mybir.dt.float32
BF16 = mybir.dt.bfloat16
I32 = mybir.dt.int32
ALU = mybir.AluOpType
ACT = mybir.ActivationFunctionType
AX = mybir.AxisListType

P = 128
B = 32
N = 256
D = 256
NT = N // P
DC = D // P
TILES = B * NT
NH = 16
DK = D // NH
H = 4
U = H + 2
EPS = 1e-5
VW = 32
SCALE1 = float(D) ** -0.5
RSQRT_SEED = float(0x5F3759DF)
NEWTON = 3
NCHAIN = 9 + 3 * NEWTON
PARTS_L = (0, 0, 1, 1, 0, 2)
PARTS_R = (0, 1, 0, 1, 2, 0)
SLOT = 64
SU = 6 * U
CO = 2 * H + 2
SC = 6 * CO

COLS = {}
_n = 0
for _name, _w in (("w1", 2), ("b1", 2), ("w2", 2), ("b2", 2), ("w3", 2), ("b3", 2), ("g1", 2), ("g2", 2),
                  ("even", 1), ("odd", 1), ("fc1b", H), ("a5", DC * (H + 1)), ("fc1", DC * H)):
    COLS[_name] = (_n, _n + _w)
    _n += _w
NPAR = _n


def build(nc, x, ctx, x0t, c0t, wqt, wkt, wvt, params, out):
    stack = ExitStack()

    def sb(name, shape, dt=F32):
        return stack.enter_context(nc.sbuf_tensor(name, shape, dt))

    def sem(name):
        return stack.enter_context(nc.semaphore(name))

    bank = [stack.enter_context(nc.psum_tensor(f"bank{i}", [P, 512], F32)) for i in range(8)]

    def tiles(ap, w=256):
        return ap[:, 0:2 * w].rearrange("p (a b) -> p a b", a=2)

    par = sb("par", [P, NPAR])
    ident = sb("ident", [P, P])
    identb = sb("identb", [P, P], BF16)
    sel = sb("sel", [4, 4 * P], BF16)
    meanw = sb("meanw", [P, P])
    scalew = sb("scalew", [P, P])
    x0T, c0T = sb("x0T", [P, DC, N]), sb("c0T", [P, DC, N])
    wqT, wkT, wvT = (sb(n, [P, DC, D]) for n in ("wqT", "wkT", "wvT"))
    qT = sb("qT", [P, 2, N])
    kTm = sb("kTm", [P, 2, 2, N])
    v1 = sb("v1", [P, NT, NH, VW])
    hmax = sb("hmax", [P, 2, NT])
    hsum = sb("hsum", [P, NT, NH])
    tgt2 = sb("tgt2", [P, NT, D])
    cN, xN = sb("cN", [P, 4, NT * D]), sb("xN", [P, 4, NT * D])
    zc, zy = sb("zc", [P, 4, NT * D]), sb("zy", [P, 4, NT * D])
    bn = sb("bn", [P, 2, 2, 4, 6])
    mv = sb("mv", [P, 3, 8])
    nmean = sb("nmean", [P, 2, 8])
    rstd = sb("rstd", [P, 2, 8])
    nwt = sb("nwt", [P, 2, 8])
    vps = sb("vps", [P, 2, 8])
    XT, FT = sb("XT", [P, 2, DC, N]), sb("FT", [P, 2, DC, N])
    Fall = sb("Fall", [P, B * DC * N])
    nmax = sb("nmax", [P, 2, NT])
    E = sb("E", [P, 2, NT * N])
    PT = sb("PT", [P, 2, NT * N])
    V1 = sb("V1", [P, 4, NT, H + 1])
    OA = sb("OA", [P, B, NT * (H + 1)])
    a5c = sb("a5c", [P, DC, H + 1])
    MT = sb("MT", [P, DC, U])
    prodQ = sb("prodQ", [P, DC, (H + 1) ** 2])
    prodK = sb("prodK", [P, DC, U * U])
    Q = sb("Q", [P, (H + 1) ** 2])
    K = sb("K", [P, U * U])
    rA = sb("rA", [P, TILES])
    hpre = sb("hpre", [P, TILES, H])
    ha = sb("ha", [P, TILES, H + 1])
    big = sb("big", [P, TILES * U * U])
    W5 = sb("W5", [P, TILES, H + 1])
    var = sb("var", [P, TILES])
    r3 = sb("r3", [P, TILES])
    t3 = sb("t3", [P, TILES])
    u = sb("u", [P, B, NT * U])
    uK = sb("uK", [P, TILES, U])
    w1s, b1s = sb("w1s", [P, DC]), sb("b1s", [P, DC])
    fc1s = sb("fc1s", [P, DC, H])
    g12 = sb("g12", [P, DC])
    cut = sb("cut", [P, TILES, CO])
    cutp = sb("cutp", [P, TILES, CO], BF16)
    stU = sb("stU", [P, B, 2, NT, SU], BF16)
    stC = sb("stC", [P, B, NT, SLOT], BF16)
    co = sb("co", [P, TILES, CO])
    Rt = sb("Rt", [P, DC, CO])
    Rcut = sb("Rcut", [P, DC, CO])
    Rp = sb("Rp", [P, DC, CO], BF16)
    stR = sb("stR", [P, DC, 2, SLOT], BF16)
    RT = sb("RT", [P, DC * P], BF16)
    sU = sb("sU", [P, 2, 2, NT, 2, SLOT], BF16)
    sT = sb("sT", [P, 2, 2 * NT * P], BF16)
    nm2 = sb("nm2", [P, 2, 2 * NT], BF16)
    nm2T = sb("nm2T", [4, 2, P], BF16)
    PT2 = sb("PT2", [P, 2, 2, NT * N])
    uS = sb("uS", [P, 2, 2, NT, VW])
    o2T = sb("o2T", [P, N])
    OB = sb("OB", [P, B, NT * U])
    rB = sb("rB", [P, TILES])
    sC = sb("sC", [P, 2, NT, 2, SLOT], BF16)
    cT = sb("cT", [P, 2, NT * P], BF16)
    fin = sb("fin", [P, 4, DC * N])
    oT = fin[:, 0:2, :]

    def c_(name, i=None, w=None):
        a, b = COLS[name]
        return par[:, a:b] if i is None else par[:, a + i:a + i + 1]

    par_in, q_in, k_in, v_in = sem("par_in"), sem("q_in"), sem("k_in"), sem("v_in")
    consts = sem("consts")
    q_mm, k_mm, v_mm = sem("q_mm"), sem("k_mm"), sem("v_mm")
    qT_ok, kT_ok, v1_ok = sem("qT_ok"), sem("kT_ok"), sem("v1_ok")
    s0_mm, max0_ok, exp0_ok = sem("s0_mm"), sem("max0_ok"), sem("exp0_ok")
    p0_mm, o0_mm = sem("p0_mm"), sem("o0_mm")
    oT_ok = [sem("oT_first"), sem("oT_second")]
    ot_mm = sem("ot_mm")
    pt0_ok = [sem("pt0_even"), sem("pt0_odd")]
    hsum_ok, tgt2_ok = sem("hsum_ok"), sem("tgt2_ok")
    c_in = [sem(f"c_in{j}") for j in range(4)]
    x_in = [sem(f"x_in{j}") for j in range(4)]
    y_ok, bn_ok = sem("y_ok"), sem("bn_ok")
    stat_ok, z_ok = sem("stat_ok"), sem("z_ok")
    xt_mm, yt_mm, XT_ok, FT_ok = sem("xt_mm"), sem("yt_mm"), sem("XT_ok"), sem("FT_ok")
    f_saved = [sem(f"f_saved{j}") for j in range(2)]
    s_mm, v_mm1, max_ok, exp_ok = sem("s_mm"), sem("v_mm1"), sem("max_ok"), sem("exp_ok")
    V1_ok, p_mm, PT_ok, o_mm, o_saved = sem("V1_ok"), sem("p_mm"), sem("PT_ok"), sem("o_mm"), sem("o_saved")
    alg = sem("alg")
    mean_mm, qk_mm, gelu_ok = sem("mean_mm"), sem("qk_mm"), sem("gelu_ok")
    r_mm, rt_ok, zero_ok = sem("r_mm"), sem("rt_ok"), sem("zero_ok")
    sU_ok, st_mm, sT_ok = sem("sU_ok"), sem("st_mm"), sem("sT_ok")
    s2_mm, max2_ok, m_mm, m_ok, s2m_mm = sem("s2_mm"), sem("max2_ok"), sem("m_mm"), sem("m_ok"), sem("s2m_mm")
    exp2_ok, o2_mm, o2_saved = sem("exp2_ok"), sem("o2_mm"), sem("o2_saved")
    uS_ok, o2T_ok, back_mm = sem("uS_ok"), sem("o2T_ok"), sem("back_mm")
    sC_ok, ct_mm, cT_ok, f_mm, fin_ok = sem("sC_ok"), sem("ct_mm"), sem("cT_ok"), sem("f_mm"), sem("fin_ok")
    out_done = [sem(f"out_done{j}") for j in range(4)]

    x_d = x.rearrange("b (p t) d -> b p (t d)", t=NT)
    c_d = ctx.rearrange("b (p t) d -> b p (t d)", t=NT)
    out_d = out.rearrange("b p c n -> b p (c n)")

    def phase(eng, step, first, last, g0, g1):
        for i in range(first, 4 * g0):
            step(i, i % 4, i // 4)
        with eng.Fori(g0, g1) as g:
            for j in range(4):
                step(g * 4 + j, j, g)
        for i in range(4 * g1, last):
            step(i, i % 4, i // 4)

    PAIRS = B // 2

    def phase2(eng, step, last):
        for p in range(4):
            step(p, p % 2)
        with eng.Fori(2, PAIRS // 2 - 2) as g:
            step(g * 2, 0)
            step(g * 2 + 1, 1)
        for p in range(PAIRS - 4, last):
            step(p, p % 2)

    def paired(p, k):
        return not isinstance(p, int) or 0 <= p + k < PAIRS

    def live(i, k):
        return not isinstance(i, int) or 0 <= i + k < B

    def later(i, k):
        return not isinstance(i, int) or i + k >= 0

    ALG = {}

    block = stack.enter_context(nc.Block())

    @block.sync
    def _(sp):
        sp.dma_start(par[:, :], params).then_inc(par_in, 16)
        for dst, src, arrived in ((x0T, x0t, q_in), (wqT, wqt, q_in), (c0T, c0t, k_in), (wkT, wkt, k_in),
                                  (wvT, wvt, v_in)):
            sp.dma_start(dst[:, :, :], src).then_inc(arrived, 16)

        def step(i, j, g):
            if live(i, 6):
                slot = (j + 6) % 4
                if later(i, 2):
                    sp.wait_ge(z_ok, 4 * (i + 3))
                sp.dma_start(cN[:, slot, :], c_d[i + 6, :, :]).then_inc(c_in[slot], 16)
                sp.dma_start(xN[:, slot, :], x_d[i + 6, :, :]).then_inc(x_in[slot], 16)
            if live(i, 1):
                sp.wait_ge(FT_ok, 2 * (i + 2))
                sp.dma_start(Fall[:, bass.ds((i + 1) * (DC * N), DC * N)],
                             FT[:, (j + 1) % 2, :, :].rearrange("p c n -> p (c n)"))\
                    .then_inc(f_saved[(j + 1) % 2], 16)

        phase(sp, step, -6, B, 1, 6)
        for s in f_saved:
            sp.wait_ge(s, 16 * (B // 2))

        def store(g):
            for j in range(4):
                sp.wait_ge(fin_ok, g * 4 + j + 1)
                sp.dma_start(out_d[g * 4 + j, :, :], fin[:, j, :]).then_inc(out_done[j], 16)

        with sp.Fori(0, B // 4) as g:
            store(g)
        for s in out_done:
            sp.wait_ge(s, 16 * (B // 4))

    @block.gpsimd
    def _(pool):
        pool.memset(ident[:, :], 0.0).then_inc(consts, 1)
        pool.memset(identb[:, :], 0.0).then_inc(consts, 1)
        pool.memset(sel[:, :], 0.0).then_inc(consts, 1)
        pool.wait_ge(consts, 3)
        pool.affine_select(out=ident[:, :], in_=ident[:, :], compare_op=ALU.not_equal, fill=1.0, base=0,
                           pattern=[[-1, P]], channel_multiplier=1).then_inc(consts, 1)
        pool.affine_select(out=identb[:, :], in_=identb[:, :], compare_op=ALU.not_equal, fill=1.0, base=0,
                           pattern=[[-1, P]], channel_multiplier=1).then_inc(consts, 1)
        pool.affine_select(out=sel[:, :], in_=sel[:, :], compare_op=ALU.not_equal, fill=1.0, base=0,
                           pattern=[[-1, 4], [0, P]], channel_multiplier=1).then_inc(consts, 1)
        pool.memset(meanw[:, :], 1.0 / D).then_inc(consts, 1)
        pool.memset(scalew[:, :], SCALE1).then_inc(consts, 1)
        pool.memset(v1[:, :, :, DK:DK + 1], 1.0).then_inc(consts, 1)
        pool.memset(V1[:, :, :, H:H + 1], 1.0).then_inc(consts, 1)
        pool.memset(v1[:, :, :, DK + 1:VW], 0.0).then_inc(consts, 1)
        pool.memset(sU[:, :, :, :, :, :], 0.0).then_inc(zero_ok, 1)
        pool.memset(stC[:, :, :, :], 0.0).then_inc(zero_ok, 1)
        pool.memset(stR[:, :, :, :], 0.0).then_inc(zero_ok, 1)
        pool.memset(ha[:, :, H:H + 1], 1.0).then_inc(zero_ok, 1)
        pool.memset(u[:, :, :].rearrange("p b (t u) -> p (b t) u", u=U)[:, :, U - 1:U], 1.0).then_inc(zero_ok, 1)
        pool.memset(co[:, :, CO - 1:CO], 1.0).then_inc(zero_ok, 1)
        pool.memset(uS[:, :, :, :, U:VW], 0.0).then_inc(zero_ok, 1)
        pool.memset(o2T[:, :], 0.0).then_inc(zero_ok, 1)

        def step(i, j, g):
            zslot, pair, m = (j + 3) % 4, ((j + 3) // 2) % 2, (j + 3) % 2
            if live(i, 3):
                pool.wait_ge(stat_ok, (2 * g + (j + 3) // 2 + 1) * NCHAIN)
                if later(i, -1):
                    pool.wait_ge(yt_mm, i)
            if live(i, 5):
                slot = (j + 5) % 4
                use = g * 4 + j + 5 - slot
                if isinstance(i, int) and i + 5 == 0:
                    pool.wait_ge(tgt2_ok, NT)
                pool.wait_ge(x_in[slot], use * 4 + 16)
                pool.tensor_tensor(xN[:, slot, :], xN[:, slot, :], tgt2[:, :, :].rearrange("p t d -> p (t d)"),
                                   ALU.add).then_inc(y_ok, 1)
            if live(i, 3):
                for t in range(2 * NT):
                    src, dst = ((cN, zc) if t < NT else (xN, zy))
                    cols = slice((t % NT) * D, (t % NT + 1) * D)
                    k = m * 4 + t
                    pool.tensor_scalar(dst[:, zslot, cols], src[:, zslot, cols], nmean[:, pair, k:k + 1],
                                       rstd[:, pair, k:k + 1], ALU.add, ALU.mult).then_inc(z_ok, 1)

        phase(pool, step, -5, B, 1, 6)

    @block.vector
    def _(dve):
        count = [0]

        def link(ins, name=None):
            ins.then_inc(alg, 1)
            count[0] += 1
            dve.wait_ge(alg, count[0])
            if name:
                ALG[name] = count[0]

        def cuts(v, left, part, slots, order):
            for k in range(3):
                link(dve.tensor_copy(part, v))
                if k < 2:
                    link(dve.tensor_tensor(left, v, part, ALU.subtract))
                for s, o in enumerate(order):
                    if o == k:
                        link(dve.tensor_copy(slots(s), part))
                v = left

        dve.wait_ge(par_in, 16)
        a5 = c_("a5").rearrange("p (c k) -> p c k", c=DC)
        link(dve.tensor_scalar(w1s[:, :], c_("w1"), SCALE1, None, ALU.mult))
        link(dve.tensor_scalar(b1s[:, :], c_("b1"), SCALE1, None, ALU.mult))
        link(dve.tensor_scalar(fc1s[:, :, :], c_("fc1").rearrange("p (c k) -> p c k", c=DC), 1.0 / SCALE1, None,
                               ALU.mult), "scaled")
        dve.wait_ge(mean_mm, 1)
        link(dve.tensor_tensor(a5c[:, :, :], a5, bank[6][:, 0:H + 1].unsqueeze(1).to_broadcast([P, DC, H + 1]),
                               ALU.subtract))
        for c in range(DC):
            link(dve.tensor_scalar(MT[:, c, 0:H + 1], a5c[:, c, :], c_("w3", c), None, ALU.mult))
            link(dve.tensor_copy(MT[:, c, U - 1:U], c_("b3", c)))
        for dst, src, n in ((prodQ, a5c, H + 1), (prodK, MT, U)):
            for c in range(DC):
                link(dve.tensor_tensor(dst[:, c, :].rearrange("p (i j) -> p i j", i=n),
                                       src[:, c, :].unsqueeze(2).to_broadcast([P, n, n]),
                                       src[:, c, :].unsqueeze(1).to_broadcast([P, n, n]), ALU.mult), "prods")
        dve.wait_ge(k_mm, 1)
        for e, m in enumerate(("even", "odd")):
            dve.tensor_scalar(kTm[:, e, :, :], tiles(bank[1]), c_(m), None, ALU.mult).then_inc(kT_ok, 1)
        dve.wait_ge(qk_mm, 1)
        link(dve.tensor_copy(Q[:, :], bank[7][:, 0:(H + 1) ** 2]))
        link(dve.tensor_copy(K[:, :], bank[7][:, 64:64 + U * U]), "QK")
        for h in range(NH + 1):
            if h < NH:
                dve.wait_ge(s0_mm, h + 1)
                if h >= 2:
                    dve.wait_ge(exp0_ok, 2 * (h - 1))
                dve.tensor_reduce(hmax[:, h % 2, :], tiles(bank[3 + h % 2]), AX.X, ALU.max, negate=True)\
                    .then_inc(max0_ok, 1)
            if h >= 1 and (h - 1) % 2 == 1:
                dve.wait_ge(p0_mm, h)
                if h >= 3:
                    dve.wait_ge(o0_mm, h - 2)
                dve.tensor_copy(PT[:, (h - 1) % 2, :], bank[5 + (h - 1) % 2][:, :]).then_inc(pt0_ok[1], 1)
        dve.wait_ge(o0_mm, NH)
        dve.tensor_copy(oT[:, 1, :], bank[1][:, :]).then_inc(oT_ok[1], 1)
        dve.wait_ge(ot_mm, 1)
        for t in range(NT):
            o = bank[5 + t][:, :].rearrange("p (h k) -> p h k", h=NH)
            dve.reciprocal(hsum[:, t, :].unsqueeze(2), o[:, :, DK:DK + 1]).then_inc(hsum_ok, 1)
        for t in range(NT):
            o = bank[5 + t][:, :].rearrange("p (h k) -> p h k", h=NH)
            dve.wait_ge(hsum_ok, t + 1)
            dve.tensor_tensor(tgt2[:, t, :].rearrange("p (h k) -> p h k", h=NH), o[:, :, 0:DK],
                              hsum[:, t, :].unsqueeze(2).to_broadcast([P, NH, DK]), ALU.mult).then_inc(tgt2_ok, 1)

        def rsqrt(v, y, t, chain):
            chain(dve.tensor_scalar(y.bitcast(I32), v.bitcast(I32), 1, None, ALU.logical_shift_right))
            chain(dve.tensor_scalar(y.bitcast(I32), y.bitcast(I32), -1.0, RSQRT_SEED, ALU.mult, ALU.add))
            for _ in range(NEWTON):
                chain(dve.tensor_tensor(t, y, y, ALU.mult))
                chain(dve.scalar_tensor_tensor(t, t, -0.5, v, ALU.mult, ALU.mult))
                chain(dve.scalar_tensor_tensor(y, t, 1.5, y, ALU.add, ALU.mult))

        def output_operand(part):
            if part == 0:
                link(dve.tensor_tensor(g12[:, :], c_("g1"), c_("g2"), ALU.mult))
                for c in range(DC):
                    link(dve.tensor_scalar(Rt[:, c, 0:H], a5[:, c, 0:H], c_("g2", c), None, ALU.mult))
                    link(dve.tensor_scalar(Rt[:, c, H:CO], MT[:, c, :], g12[:, c:c + 1], None, ALU.mult))
                    link(dve.scalar_tensor_tensor(Rt[:, c, CO - 1:CO], a5[:, c, H:H + 1], c_("g2", c),
                                                  Rt[:, c, CO - 1:CO], ALU.mult, ALU.add))
                dve.wait_ge(zero_ok, 6)
            else:
                cuts(Rt[:, :, :], Rcut[:, :, :], Rp[:, :, :],
                     lambda s: stR[:, :, part - 1, s * CO:(s + 1) * CO], PARTS_L)
                ALG["stR"] = count[0]

        def step(i, j, g):
            if isinstance(i, int) and 1 <= i <= 3:
                output_operand(i - 1)
            if live(i, 4):
                slot, pr, m = j, (j // 2) % 2, j % 2
                dve.wait_ge(c_in[slot], g * 16 + 32)
                dve.wait_ge(y_ok, i + 5)
                for t in range(2 * NT):
                    src = cN if t < NT else xN
                    dve.bn_stats(bn[:, pr, m, t, :], src[:, slot, (t % NT) * D:(t % NT + 1) * D]).then_inc(bn_ok, 1)
                if m == 1:
                    done = [(2 * g + (j + 4) // 2) * NCHAIN]

                    def inc(ins):
                        ins.then_inc(stat_ok, 1)
                        done[0] = done[0] + 1

                    def chain(ins):
                        inc(ins)
                        dve.wait_ge(stat_ok, done[0])

                    half = bn[:, pr, :, :, :].rearrange("p m t s -> p (m t) s")
                    total, apart, squares = (mv[:, k, :].unsqueeze(2) for k in range(3))
                    if later(i, 0):
                        dve.wait_ge(z_ok, 4 * (i + 1))
                    dve.wait_ge(bn_ok, 4 * (i + 5))
                    inc(dve.tensor_tensor(apart, half[:, :, 1:2], half[:, :, 4:5], ALU.subtract))
                    inc(dve.tensor_tensor(total, half[:, :, 1:2], half[:, :, 4:5], ALU.add))
                    chain(dve.tensor_tensor(squares, half[:, :, 2:3], half[:, :, 5:6], ALU.add))
                    inc(dve.tensor_scalar(nmean[:, pr, :], mv[:, 0, :], -0.5, None, ALU.mult))
                    chain(dve.tensor_tensor(apart, apart, apart, ALU.mult))
                    chain(dve.scalar_tensor_tensor(vps[:, pr, :], mv[:, 1, :], D / 4.0, mv[:, 2, :], ALU.mult, ALU.add))
                    chain(dve.tensor_scalar(vps[:, pr, :], vps[:, pr, :], 1.0 / D, EPS, ALU.mult, ALU.add))
                    rsqrt(vps[:, pr, :], rstd[:, pr, :], nwt[:, pr, :], chain)
            if live(i, 0):
                dve.wait_ge(s_mm, i + 1)
                if later(i, -2):
                    dve.wait_ge(exp_ok, 2 * i - 2)
                dve.tensor_reduce(nmax[:, j % 2, :], tiles(bank[2 + j % 2]), AX.X, ALU.max, negate=True)\
                    .then_inc(max_ok, 1)
                dve.wait_ge(v_mm1, i + 1)
                if later(i, -4):
                    dve.wait_ge(o_mm, i - 3)
                dve.tensor_copy(V1[:, j, :, 0:H], bank[6][:, 0:NT * H].rearrange("p (t h) -> p t h", t=NT))\
                    .then_inc(V1_ok, 1)
            if live(i, -2):
                dve.wait_ge(o_mm, i - 1)
                dve.tensor_copy(OA[:, bass.ds(i - 2, 1), :], bank[7][:, 0:NT * (H + 1)].unsqueeze(1)).then_inc(o_saved, 1)

        phase(dve, step, -4, B + 2, 1, 7)

        def spread(ap, w):
            return ap.unsqueeze(2).to_broadcast([P, TILES, w])

        def quadratic(dst, v, m, n):
            w = big[:, 0:TILES * n * n].rearrange("p (t j i) -> p t j i", t=TILES, j=n)
            link(dve.tensor_tensor(w, v.unsqueeze(2).to_broadcast([P, TILES, n, n]),
                                   m.rearrange("p (j i) -> p j i", j=n).unsqueeze(1).to_broadcast([P, TILES, n, n]),
                                   ALU.mult))
            link(dve.tensor_reduce(dst, w, AX.X, ALU.add))

        dve.wait_ge(o_saved, B)
        oa = OA[:, :, :].rearrange("p b (t k) -> p (b t) k", t=NT)
        ut = u[:, :, :].rearrange("p b (t k) -> p (b t) k", t=NT)
        link(dve.reciprocal(rA[:, :].unsqueeze(2), oa[:, :, H:H + 1]))
        link(dve.tensor_tensor(hpre[:, :, :], oa[:, :, 0:H], spread(rA[:, :], H), ALU.mult))
        link(dve.tensor_tensor(hpre[:, :, :], hpre[:, :, :], c_("fc1b").unsqueeze(1).to_broadcast([P, TILES, H]),
                               ALU.add), "hpre")
        dve.wait_ge(gelu_ok, 1)
        quadratic(W5[:, :, :], ha[:, :, :], Q[:, :], H + 1)
        link(dve.tensor_tensor(W5[:, :, :], W5[:, :, :], ha[:, :, :], ALU.mult))
        link(dve.tensor_reduce(var[:, :], W5[:, :, :], AX.X, ALU.add))
        link(dve.tensor_scalar(var[:, :], var[:, :], EPS, None, ALU.add))
        rsqrt(var[:, :], r3[:, :], t3[:, :], link)
        link(dve.tensor_tensor(ut[:, :, 0:H + 1], ha[:, :, :], spread(r3[:, :], H + 1), ALU.mult), "u")
        quadratic(uK[:, :, :], ut, K[:, :], U)
        for side, v, order in ((0, uK[:, :, :], PARTS_L), (1, ut, PARTS_R)):
            cuts(v, cut[:, :, 0:U], cutp[:, :, 0:U],
                 lambda s: stU[:, :, side, :, s * U:(s + 1) * U], order)
        ALG["stU"] = count[0]

        def turned(p, r):
            dve.wait_ge(st_mm, p + 1)
            if not isinstance(p, int) or p >= 2:
                dve.wait_ge(s2_mm, p * 2 - 2)
            dve.tensor_copy(sT[:, r, :], bank[4][:, 0:NT * P].bitcast(BF16)).then_inc(sT_ok, 1)

        def maxima(p, r):
            if not isinstance(p, int) or p >= 2:
                dve.wait_ge(m_mm, p - 1)
            for m in range(2):
                dve.wait_ge(s2_mm, p * 2 + (m + 1))
                dve.tensor_reduce(nm2[:, r, NT * m:NT * (m + 1)], tiles(bank[2 * r + m]), AX.X, ALU.max,
                                  negate=True).then_inc(max2_ok, 1)

        def step2(p, r):
            if paired(p, 1):
                maxima(p + 1, 1 - r)
            if paired(p, 2):
                turned(p + 2, r)
            if paired(p, -2):
                dve.wait_ge(back_mm, p - 1)
                dve.tensor_copy(OB[:, bass.ds(p * 2 - 4, 2), :].rearrange("p m (t k) -> p m t k", t=NT),
                                bank[7][:, 0:NT * P].rearrange("p (t m k) -> p m t k", t=NT, k=VW)[:, 0:2, :, 0:U])\
                    .then_inc(o2_saved, 1)
            if paired(p, -1):
                dve.wait_ge(o2_mm, p)
                dve.tensor_copy(o2T[0:2 * VW, :], bank[6][0:2 * VW, 0:N]).then_inc(o2T_ok, 1)

        dve.wait_ge(zero_ok, 8)
        turned(0, 0)
        maxima(0, 0)
        turned(1, 1)
        phase2(dve, step2, PAIRS + 2)

        dve.wait_ge(o2_saved, B // 2)
        ob = OB[:, :, :].rearrange("p b (t k) -> p (b t) k", t=NT)
        link(dve.reciprocal(rB[:, :].unsqueeze(2), ob[:, :, U - 1:U]))
        link(dve.tensor_tensor(co[:, :, H:CO - 1], ob[:, :, 0:H + 1], spread(rB[:, :], H + 1), ALU.mult))
        link(dve.tensor_copy(co[:, :, 0:H], ha[:, :, 0:H]))
        cuts(co[:, :, :].rearrange("p (b t) k -> p b t k", t=NT), cut[:, :, :].rearrange("p (b t) k -> p b t k", t=NT),
             cutp[:, :, :].rearrange("p (b t) k -> p b t k", t=NT), lambda s: stC[:, :, :, s * CO:(s + 1) * CO], PARTS_R)
        ALG["stC"] = count[0]

        def results(g, first=False):
            for j in range(4):
                dve.wait_ge(f_mm, g * 4 + (j + 1))
                if not first:
                    dve.wait_ge(out_done[j], g * 16)
                dve.tensor_tensor(fin[:, j, :], bank[j][:, :],
                                  Fall[:, bass.ds(g * (4 * DC * N) + j * DC * N, DC * N)], ALU.add).then_inc(fin_ok, 1)

        results(0, first=True)
        with dve.Fori(1, B // 4) as g:
            results(g)

    @block.scalar
    def _(act):
        act.wait_ge(q_mm, 1)
        act.activation(qT[:, :, :], tiles(bank[0]), ACT.Copy, scale=float(DK) ** -0.5).then_inc(qT_ok, 1)
        act.wait_ge(v_mm, 1)
        act.wait_ge(consts, 9)
        for t in range(NT):
            act.activation(v1[:, t, :, 0:DK], bank[2][:, t * D:(t + 1) * D].rearrange("p (h k) -> p h k", h=NH),
                           ACT.Copy).then_inc(v1_ok, 1)
        for h in range(NH + 1):
            if h == 12:
                act.wait_ge(o0_mm, NH // 2)
                act.activation(oT[:, 0, :], bank[0][:, :], ACT.Copy).then_inc(oT_ok[0], 1)
            if h < NH:
                act.wait_ge(max0_ok, h + 1)
                if h >= 2:
                    act.wait_ge(p0_mm, h - 1)
                for t in range(NT):
                    act.activation(E[:, h % 2, t * N:(t + 1) * N], bank[3 + h % 2][:, t * N:(t + 1) * N], ACT.Exp,
                                   bias=hmax[:, h % 2, t:t + 1]).then_inc(exp0_ok, 1)
            if h >= 1 and (h - 1) % 2 == 0:
                act.wait_ge(p0_mm, h)
                if h >= 3:
                    act.wait_ge(o0_mm, h - 2)
                act.activation(PT[:, (h - 1) % 2, :], bank[5 + (h - 1) % 2][:, :], ACT.Copy).then_inc(pt0_ok[0], 1)

        def step(i, j, g):
            n = (j + 1) % 2
            if live(i, 1):
                act.wait_ge(yt_mm, i + 2)
                if later(i, -1):
                    act.wait_ge(s_mm, i)
                    act.wait_ge(f_saved[n], (g * 4 + j + 1 - n) * 8)
                for c in range(DC):
                    act.activation(FT[:, n, c, :], bank[1][:, c * N:(c + 1) * N], ACT.Identity,
                                   bias=c_("b2", c), scale=c_("w2", c)).then_inc(FT_ok, 1)
                if later(i, -1):
                    act.wait_ge(v_mm1, i)
                for c in range(DC):
                    act.activation(XT[:, n, c, :], bank[0][:, c * N:(c + 1) * N], ACT.Identity,
                                   bias=b1s[:, c:c + 1], scale=w1s[:, c:c + 1]).then_inc(XT_ok, 1)
            if live(i, 0):
                act.wait_ge(max_ok, i + 1)
                if later(i, -2):
                    act.wait_ge(p_mm, i - 1)
                for t in range(NT):
                    act.activation(E[:, j % 2, t * N:(t + 1) * N], bank[2 + j % 2][:, t * N:(t + 1) * N], ACT.Exp,
                                   bias=nmax[:, j % 2, t:t + 1]).then_inc(exp_ok, 1)
            if live(i, -1):
                act.wait_ge(p_mm, i)
                if later(i, -3):
                    act.wait_ge(o_mm, i - 2)
                act.activation(PT[:, n, :], bank[4 + n][:, :], ACT.Copy).then_inc(PT_ok, 1)

        phase(act, step, -1, B + 1, 1, 7)

        act.wait_ge(r_mm, 1)
        act.activation(RT[:, :], bank[5][:, 0:DC * P // 2].bitcast(BF16), ACT.Copy).then_inc(rt_ok, 1)

        act.wait_ge(alg, ALG["hpre"])
        act.activation(ha[:, :, 0:H], hpre[:, :, :], ACT.Gelu).then_inc(gelu_ok, 1)

        def copy(p, r):
            for m in range(2):
                act.activation(sU[:, r, :, :, m, 0:SU], stU[:, bass.ds(p * 2 + m, 1), :, :, :],
                               ACT.Copy).then_inc(sU_ok, 1)

        def maxima_turned(p, r):
            act.wait_ge(m_mm, p + 1)
            if not isinstance(p, int) or p >= 2:
                act.wait_ge(s2m_mm, p * 2 - 2)
            act.activation(nm2T[:, r, :], bank[5][0:4, 0:P // 2].bitcast(BF16), ACT.Copy).then_inc(m_ok, 1)

        def step2(p, r):
            for m in range(2):
                act.wait_ge(s2m_mm, p * 2 + (m + 1))
                if not isinstance(p, int) or p >= 2:
                    act.wait_ge(o2_mm, p - 1)
                act.activation(PT2[:, r, m, :], bank[2 * r + m][:, :], ACT.Exp).then_inc(exp2_ok, 1)
            act.activation(uS[:, r, :, :, 0:U], u[:, bass.ds(p * 2, 2), :].rearrange("p m (t k) -> p m t k", t=NT),
                           ACT.Copy).then_inc(uS_ok, 1)
            if paired(p, 3):
                act.wait_ge(st_mm, p + 2)
                copy(p + 3, 1 - r)
            if paired(p, 1):
                maxima_turned(p + 1, 1 - r)

        act.wait_ge(zero_ok, 6)
        act.wait_ge(alg, ALG["stU"])
        copy(0, 0)
        copy(1, 1)
        act.wait_ge(st_mm, 1)
        copy(2, 0)
        maxima_turned(0, 0)
        phase2(act, step2, PAIRS)

        def copy3(p, r):
            act.activation(sC[:, r, :, :, :], stC[:, bass.ds(p * 2, 2), :, :].rearrange("p b t r -> p t b r"),
                           ACT.Copy).then_inc(sC_ok, 1)

        def pair3(p, r, first=False, ahead=True):
            act.wait_ge(ct_mm, p + 1)
            if not first:
                act.wait_ge(f_mm, p * 2 - 2)
            act.activation(cT[:, r, :], bank[4 + r][:, 0:NT * P // 2].bitcast(BF16), ACT.Copy).then_inc(cT_ok, 1)
            if ahead:
                copy3(p + 2, r)

        act.wait_ge(alg, ALG["stC"])
        copy3(0, 0)
        copy3(1, 1)
        pair3(0, 0, first=True)
        pair3(1, 1, first=True)
        with act.Fori(1, B // 4 - 1) as g:
            pair3(g * 2, 0)
            pair3(g * 2 + 1, 1)
        pair3(B // 2 - 2, 0, ahead=False)
        pair3(B // 2 - 1, 1, ahead=False)

    @block.tensor
    def _(pe):
        pe.wait_ge(par_in, 16)
        pe.wait_ge(consts, 8)
        a5 = c_("a5").rearrange("p (c k) -> p c k", c=DC)
        for c in range(DC):
            last = pe.matmul(bank[6][:, 0:H + 1], meanw[:, :], a5[:, c, :], start=c == 0, stop=c == DC - 1)
        last.then_inc(mean_mm, 1)
        for arrived, n, w, src, b, done in ((q_in, 32, wqT, x0T, 0, q_mm), (k_in, 32, wkT, c0T, 1, k_mm)):
            pe.wait_ge(arrived, n)
            for o in range(2):
                for c in range(DC):
                    last = pe.matmul(bank[b][:, o * N:(o + 1) * N], w[:, c, o * P:(o + 1) * P], src[:, c, :],
                                     start=c == 0, stop=c == DC - 1)
            last.then_inc(done, 1)
        pe.wait_ge(v_in, 16)
        for t in range(NT):
            for c in range(DC):
                last = pe.matmul(bank[2][:, t * D:(t + 1) * D], c0T[:, c, t * P:(t + 1) * P], wvT[:, c, :],
                                 start=c == 0, stop=c == DC - 1)
        last.then_inc(v_mm, 1)
        pe.wait_ge(alg, ALG["prods"])
        for dst, w, src, n in ((0, meanw, prodQ, (H + 1) ** 2), (64, scalew, prodK, U * U)):
            for c in range(DC):
                last = pe.matmul(bank[7][:, dst:dst + n], w[:, :], src[:, c, :], start=c == 0, stop=c == DC - 1)
        last.then_inc(qk_mm, 1)

        pe.wait_ge(qT_ok, 1)
        pe.wait_ge(kT_ok, 2)
        for h in range(NH + 2):
            if h < NH:
                o, q, e = h // 8, 32 * ((h % 8) // 2), h % 2
                if h >= 2:
                    pe.wait_ge(exp0_ok, 2 * (h - 1))
                for t in range(NT):
                    last = pe.matmul(bank[3 + h % 2][:, t * N:(t + 1) * N], qT[q:q + 32, o, t * P:(t + 1) * P],
                                     kTm[q:q + 32, e, o, :], start=True, stop=True)
                last.then_inc(s0_mm, 1)
            if 1 <= h <= NH:
                pe.wait_ge(exp0_ok, 2 * h)
                if h >= 3:
                    pe.wait_ge(pt0_ok[(h - 1) % 2], (h - 1) // 2)
                n = (h - 1) % 2
                for k in range(NT):
                    for t in range(NT):
                        last = pe.transpose(bank[5 + n][:, k * N + t * P:k * N + (t + 1) * P],
                                            E[:, n, t * N + k * P:t * N + (k + 1) * P], ident[:, :])
                last.then_inc(p0_mm, 1)
            if h >= 2:
                if h == 2:
                    pe.wait_ge(v1_ok, 2)
                    pe.wait_ge(consts, 11)
                pe.wait_ge(pt0_ok[h % 2], h // 2)
                group, row = (h - 2) // 4, VW * ((h - 2) % 4)
                for k in range(NT):
                    last = pe.matmul(bank[group // 2][row:row + VW, (group % 2) * N:(group % 2 + 1) * N],
                                     v1[:, k, h - 2, :], PT[:, h % 2, k * N:(k + 1) * N],
                                     start=k == 0, stop=k == NT - 1, skip_group_check=True)
                last.then_inc(o0_mm, 1)
        for group in range(NH // 4):
            pe.wait_ge(oT_ok[group // 2], 1)
            for t in range(NT):
                last = pe.transpose(bank[5 + t][:, group * P:(group + 1) * P],
                                    oT[:, group // 2, (group % 2) * N + t * P:(group % 2) * N + (t + 1) * P], ident[:, :])
        last.then_inc(ot_mm, 1)

        fc1 = fc1s
        def step(i, j, g):
            n = (j + 1) % 2
            if live(i, 1):
                pe.wait_ge(z_ok, 4 * (i + 2))
                if later(i, 0):
                    pe.wait_ge(XT_ok, 2 * (i + 1))
                    pe.wait_ge(FT_ok, 2 * (i + 1))
                for b, z, done in ((0, zc, xt_mm), (1, zy, yt_mm)):
                    for c in range(DC):
                        for t in range(NT):
                            last = pe.transpose(bank[b][:, c * N + t * P:c * N + (t + 1) * P],
                                                z[:, (j + 1) % 4, t * D + c * P:t * D + (c + 1) * P], ident[:, :])
                    last.then_inc(done, 1)
            if live(i, 0):
                pe.wait_ge(FT_ok, 2 * (i + 1))
                pe.wait_ge(XT_ok, 2 * (i + 1))
                if later(i, -2):
                    pe.wait_ge(exp_ok, 2 * i - 2)
                for t in range(NT):
                    for c in range(DC):
                        last = pe.matmul(bank[2 + j % 2][:, t * N:(t + 1) * N], FT[:, j % 2, c, t * P:(t + 1) * P],
                                         XT[:, j % 2, c, :], start=c == 0, stop=c == DC - 1)
                last.then_inc(s_mm, 1)
                if later(i, -1):
                    pe.wait_ge(V1_ok, i)
                for t in range(NT):
                    for c in range(DC):
                        last = pe.matmul(bank[6][:, t * H:(t + 1) * H], XT[:, j % 2, c, t * P:(t + 1) * P],
                                         fc1[:, c, :], start=c == 0, stop=c == DC - 1)
                last.then_inc(v_mm1, 1)
            if live(i, -1):
                pe.wait_ge(exp_ok, 2 * i)
                if later(i, -3):
                    pe.wait_ge(PT_ok, i - 2)
                for k in range(NT):
                    for t in range(NT):
                        last = pe.transpose(bank[4 + n][:, k * N + t * P:k * N + (t + 1) * P],
                                            E[:, n, t * N + k * P:t * N + (k + 1) * P], ident[:, :])
                last.then_inc(p_mm, 1)
            if live(i, -2):
                pe.wait_ge(PT_ok, i - 1)
                pe.wait_ge(V1_ok, i - 1)
                if later(i, -3):
                    pe.wait_ge(o_saved, i - 2)
                else:
                    pe.wait_ge(alg, ALG["QK"])
                for t in range(NT):
                    for k in range(NT):
                        last = pe.matmul(bank[7][:, t * (H + 1):(t + 1) * (H + 1)],
                                         PT[:, j % 2, k * N + t * P:k * N + (t + 1) * P], V1[:, (j + 2) % 4, k, :],
                                         start=k == 0, stop=k == NT - 1)
                last.then_inc(o_mm, 1)

        phase(pe, step, -1, B + 2, 1, 7)

        pe.wait_ge(PT_ok, B)
        pe.wait_ge(alg, ALG["stR"])
        for c in range(DC):
            last = pe.transpose(bank[5][:, c * P // 2:(c + 1) * P // 2].bitcast(BF16),
                                stR[:, c, :, :].rearrange("p m r -> p (m r)"), identb[:, :])
        last.then_inc(r_mm, 1)
        pe.wait_ge(rt_ok, 1)

        def turn(p, r):
            pe.wait_ge(sU_ok, p * 2 + 2)
            if not isinstance(p, int) or p >= 1:
                pe.wait_ge(sT_ok, p)
            for side in range(2):
                for t in range(NT):
                    k = (side * NT + t) * P // 2
                    last = pe.transpose(bank[4][:, k:k + P // 2].bitcast(BF16),
                                        sU[:, r, side, t, :, :].rearrange("p m r -> p (m r)"), identb[:, :])
            last.then_inc(st_mm, 1)

        def scores(p, r):
            pe.wait_ge(sT_ok, p + 1)
            if not isinstance(p, int) or p >= 2:
                pe.wait_ge(exp2_ok, p * 2 - 2)
            for m in range(2):
                rows = slice(SLOT * m, SLOT * m + SU)
                for k in range(NT):
                    last = pe.matmul(bank[2 * r + m][:, k * N:(k + 1) * N],
                                     sT[rows, r, k * P:(k + 1) * P], sT[rows, r, NT * P:2 * NT * P],
                                     start=k == 0, stop=True, skip_group_check=True)
                last.then_inc(s2_mm, 1)

        def maxima_turn(p, r):
            pe.wait_ge(max2_ok, p * 2 + 2)
            if not isinstance(p, int) or p >= 1:
                pe.wait_ge(m_ok, p)
            pe.transpose(bank[5][0:4, 0:P // 2].bitcast(BF16), nm2[:, r, :], identb[:, :]).then_inc(m_mm, 1)

        def step2(p, r):
            if paired(p, 0):
                pe.wait_ge(m_ok, p + 1)
                for m in range(2):
                    for t in range(NT):
                        last = pe.matmul(tiles(bank[2 * r + m])[:, :, t * P:(t + 1) * P],
                                         sel[:, (m * NT + t) * P:(m * NT + t + 1) * P],
                                         nm2T[:, r, :].unsqueeze(1).to_broadcast([4, NT, P]), start=False, stop=True,
                                         skip_group_check=True)
                    last.then_inc(s2m_mm, 1)
            if paired(p, 1):
                scores(p + 1, 1 - r)
            if paired(p, 2):
                turn(p + 2, r)
            if paired(p, -2):
                pe.wait_ge(o2T_ok, p - 1)
                if not isinstance(p, int) or p >= 3:
                    pe.wait_ge(o2_saved, p - 2)
                for t in range(NT):
                    last = pe.transpose(bank[7][:, t * P:(t + 1) * P], o2T[:, t * P:(t + 1) * P], ident[:, :])
                last.then_inc(back_mm, 1)
            if paired(p, -1):
                pe.wait_ge(exp2_ok, p * 2)
                pe.wait_ge(uS_ok, p)
                if not isinstance(p, int) or p >= 2:
                    pe.wait_ge(o2T_ok, p - 1)
                for m in range(2):
                    for k in range(NT):
                        last = pe.matmul(bank[6][VW * m:VW * (m + 1), 0:N], uS[:, 1 - r, m, k, :],
                                         PT2[:, 1 - r, m, k * N:(k + 1) * N], start=k == 0, stop=k == NT - 1,
                                         skip_group_check=True)
                    if m == 0 and paired(p, 1):
                        maxima_turn(p + 1, 1 - r)
                last.then_inc(o2_mm, 1)
            elif paired(p, 1):
                maxima_turn(p + 1, 1 - r)

        turn(0, 0)
        scores(0, 0)
        turn(1, 1)
        maxima_turn(0, 0)
        pe.wait_ge(zero_ok, 8)
        phase2(pe, step2, PAIRS + 2)

        def pair3(p, r, first=False, ahead=True, now=True):
            if ahead:
                pe.wait_ge(sC_ok, p + 2)
                if not first:
                    pe.wait_ge(cT_ok, p)
                for t in range(NT):
                    last = pe.transpose(bank[5 - r][:, t * P // 2:(t + 1) * P // 2].bitcast(BF16),
                                        sC[:, 1 - r, t, :, :].rearrange("p m r -> p (m r)"), identb[:, :])
                last.then_inc(ct_mm, 1)
            if now:
                pe.wait_ge(cT_ok, p + 1)
                for m in range(2):
                    rows = slice(SLOT * m, SLOT * m + SC)
                    if not isinstance(p, int) or p >= 2:
                        pe.wait_ge(fin_ok, p * 2 + m - 3)
                    for c in range(DC):
                        last = pe.matmul(bank[2 * r + m][:, c * N:(c + 1) * N], RT[rows, c * P:(c + 1) * P],
                                         cT[rows, r, :], start=True, stop=True)
                    last.then_inc(f_mm, 1)

        pair3(-1, 1, first=True, now=False)
        pair3(0, 0, first=True)
        pair3(1, 1)
        with pe.Fori(1, B // 4 - 1) as g:
            pair3(g * 2, 0)
            pair3(g * 2 + 1, 1)
        pair3(B // 2 - 2, 0)
        pair3(B // 2 - 1, 1, ahead=False)

    stack.close()


def kernel(**inputs):
    import numpy as np
    import concourse.bacc as bacc
    from concourse.bass_utils import run_bass_kernel_spmd

    a = {k: np.asarray(v) for k, v in inputs.items()}

    def columns(v):
        return v.reshape(DC, P, -1).transpose(1, 0, 2).reshape(P, -1)

    def by_feature(m):
        return m.T.reshape(DC, P, -1).transpose(1, 0, 2)

    def tokens(m):
        return m.reshape(P, NT, D).transpose(1, 0, 2).reshape(N, D)

    even = (np.arange(P) // DK % 2 == 0).astype(np.float32)
    pieces = {
        "w1": columns(a["L1_xattn_norm1_w"]), "b1": columns(a["L1_xattn_norm1_b"]),
        "w2": columns(a["L1_xattn_norm2_w"]), "b2": columns(a["L1_xattn_norm2_b"]),
        "w3": columns(a["L1_xattn_norm3_w"]), "b3": columns(a["L1_xattn_norm3_b"]),
        "g1": columns(a["L1_xattn_gamma1"]), "g2": columns(a["L1_xattn_gamma2"]),
        "even": even[:, None], "odd": np.logical_not(even)[:, None].astype(np.float32),
        "fc1b": np.broadcast_to(a["L1_xattn_fc1_b"][None, :], (P, H)),
        "a5": columns(np.concatenate([a["L1_xattn_fc2_w"], a["L1_xattn_fc2_b"][:, None]], axis=1)),
        "fc1": columns(a["L1_xattn_fc1_w"].T),
    }
    arrays = {
        "x": a["x"], "ctx": a["ctx_1024"],
        "x0t": by_feature(tokens(a["x"][0])), "c0t": by_feature(tokens(a["ctx_1024"][0])),
        "wqt": by_feature(a["L0_xattn_Wq"]), "wkt": by_feature(a["L0_xattn_Wk"]), "wvt": by_feature(a["L0_xattn_Wv"]),
        "params": np.concatenate([pieces[k] for k in COLS], axis=1),
    }
    arrays = {k: np.ascontiguousarray(v) for k, v in arrays.items()}
    nc = bacc.Bacc("TRN2", target_bir_lowering=False, num_devices=1)
    args = [nc.dram_tensor(k, v.shape, mybir.dt.from_np(v.dtype), kind="ExternalInput").ap() for k, v in arrays.items()]
    args.append(nc.dram_tensor("out", (B, P, DC, N), F32, kind="ExternalOutput").ap())
    build(nc, *args)
    got = run_bass_kernel_spmd(nc, [arrays], core_ids=[0]).results[0]["out"]
    return got.reshape(B, P, DC, NT, P).transpose(0, 4, 3, 2, 1).reshape(B, N, D)
```
